# Optimizing a Trainium2 kernel written in Bass

```python
import numpy as np
import jax
import jax.numpy as jnp

def _softmax(x, axis=-1):
    return jax.nn.softmax(x, axis=axis)

def _gelu(x):
    return jax.nn.gelu(x, approximate=True)

def _silu(x):
    return jax.nn.silu(x)

def _sigmoid(x):
    return jax.nn.sigmoid(x)

def _layernorm(x, axis=-1, eps=1e-05):
    m = jnp.mean(x, axis=axis, keepdims=True)
    v = jnp.var(x, axis=axis, keepdims=True)
    return (x - m) / jnp.sqrt(v + eps)

def _scatter_add(tgt, idx, src, axis=0):
    return tgt.at[idx].add(src)

def _segment_sum(src, seg, n):
    return jax.ops.segment_sum(src, seg, n)
kernel_name = 'mk_hybrid_d1_jaxref_r8_21788d'

def setup_inputs(seed: int=0):
    np.random.seed(seed)
    _w = jnp.asarray

    def _L0_attn_a_setup():
        import jax, jax.numpy as jnp
        import numpy as np
        DIM = 256
        N_HEADS = 32
        N_KV_HEADS = 8
        ROPE_THETA = 10000.0

        def _rope(x, theta):
            B, N, H, D = x.shape
            freq = theta ** (-(jnp.arange(D // 2, dtype=jnp.float32) * (2.0 / D)))
            phase = jnp.arange(N, dtype=jnp.float32)[:, None] * freq[None, :]
            c = jnp.cos(phase)[None, :, None, :]
            s = jnp.sin(phase)[None, :, None, :]
            x0, x1 = (x[..., 0::2], x[..., 1::2])
            return jnp.stack([x0 * c - x1 * s, x0 * s + x1 * c], axis=-1).reshape(B, N, H, D)
        key = jax.random.key(seed)
        k0, k1, k2, k3, k4 = jax.random.split(key, 5)
        B, N = (2, 128)
        kv_dim = DIM // (N_HEADS // N_KV_HEADS)
        return {'x': jax.random.normal(k0, (B, N, DIM), jnp.float32), 'wq': jax.random.normal(k1, (DIM, DIM), jnp.float32) * 0.02, 'wk': jax.random.normal(k2, (DIM, kv_dim), jnp.float32) * 0.02, 'wv': jax.random.normal(k3, (DIM, kv_dim), jnp.float32) * 0.02, 'wo': jax.random.normal(k4, (DIM, DIM), jnp.float32) * 0.02}
    _L0_attn_a_in = _L0_attn_a_setup()

    def _L0_attn_b_setup():
        import jax, jax.numpy as jnp
        import numpy as np
        N_HEADS = 16
        key = jax.random.key(seed)
        ks = jax.random.split(key, 9)
        B, S, D = (2, 256, 256)
        s = 0.02
        return {'X': jax.random.normal(ks[0], (B, S, D), jnp.float32), 'Wq': jax.random.normal(ks[1], (D, D), jnp.float32) * s, 'bq': jax.random.normal(ks[2], (D,), jnp.float32) * s, 'Wk': jax.random.normal(ks[3], (D, D), jnp.float32) * s, 'bk': jax.random.normal(ks[4], (D,), jnp.float32) * s, 'Wv': jax.random.normal(ks[5], (D, D), jnp.float32) * s, 'bv': jax.random.normal(ks[6], (D,), jnp.float32) * s, 'Wo': jax.random.normal(ks[7], (D, D), jnp.float32) * s, 'bo': jax.random.normal(ks[8], (D,), jnp.float32) * s}
    _L0_attn_b_in = _L0_attn_b_setup()

    def _L0_ffn_setup():
        import jax, jax.numpy as jnp
        import numpy as np
        HIDDEN = 256
        INTER = 1024
        BATCH, LOCAL_SEQ = (2, 512)
        key = jax.random.key(seed)
        k1, k2, k3 = jax.random.split(key, 3)
        h_shard = jax.random.normal(k1, (BATCH, LOCAL_SEQ, HIDDEN), dtype=jnp.float32)
        w_gate_up = jax.random.normal(k2, (2 * INTER, HIDDEN), dtype=jnp.float32) * 0.02
        w_down = jax.random.normal(k3, (HIDDEN, INTER), dtype=jnp.float32) * 0.02
        return {'h_shard': h_shard, 'w_gate_up': w_gate_up, 'w_down': w_down}
    _L0_ffn_in = _L0_ffn_setup()
    _d = {'L0_attn_a_x': _L0_attn_a_in['x'], 'L0_attn_a_wq': _L0_attn_a_in['wq'], 'L0_attn_a_wk': _L0_attn_a_in['wk'], 'L0_attn_a_wv': _L0_attn_a_in['wv'], 'L0_attn_a_wo': _L0_attn_a_in['wo'], 'L0_attn_b_Wq': _L0_attn_b_in['Wq'], 'L0_attn_b_bq': _L0_attn_b_in['bq'], 'L0_attn_b_Wk': _L0_attn_b_in['Wk'], 'L0_attn_b_bk': _L0_attn_b_in['bk'], 'L0_attn_b_Wv': _L0_attn_b_in['Wv'], 'L0_attn_b_bv': _L0_attn_b_in['bv'], 'L0_attn_b_Wo': _L0_attn_b_in['Wo'], 'L0_attn_b_bo': _L0_attn_b_in['bo'], 'L0_ffn_w_gate_up': _L0_ffn_in['w_gate_up'], 'L0_ffn_w_down': _L0_ffn_in['w_down']}
    _x0 = _d['L0_attn_a_x']
    _d['L0_attn_a_x'] = jax.random.normal(jax.random.fold_in(jax.random.key(seed), 1), (2, 1024, 256), dtype=_x0.dtype)
    del _x0
    return _d

def reference(L0_attn_a_x, L0_attn_a_wq, L0_attn_a_wk, L0_attn_a_wv, L0_attn_a_wo, L0_attn_b_Wq, L0_attn_b_bq, L0_attn_b_Wk, L0_attn_b_bk, L0_attn_b_Wv, L0_attn_b_bv, L0_attn_b_Wo, L0_attn_b_bo, L0_ffn_w_gate_up, L0_ffn_w_down):

    def _L0_attn_a_ref(x, wq, wk, wv, wo):
        import jax, jax.numpy as jnp
        import numpy as np
        DIM = 256
        N_HEADS = 32
        N_KV_HEADS = 8
        ROPE_THETA = 10000.0

        def _rope(x, theta):
            B, N, H, D = x.shape
            freq = theta ** (-(jnp.arange(D // 2, dtype=jnp.float32) * (2.0 / D)))
            phase = jnp.arange(N, dtype=jnp.float32)[:, None] * freq[None, :]
            c = jnp.cos(phase)[None, :, None, :]
            s = jnp.sin(phase)[None, :, None, :]
            x0, x1 = (x[..., 0::2], x[..., 1::2])
            return jnp.stack([x0 * c - x1 * s, x0 * s + x1 * c], axis=-1).reshape(B, N, H, D)
        B, N, D = x.shape
        H, J = (N_HEADS, N_KV_HEADS)
        hd = D // H
        q = (x @ wq).reshape(B, N, H, hd)
        k = (x @ wk).reshape(B, N, J, hd)
        v = (x @ wv).reshape(B, N, J, hd)
        q = _rope(q, ROPE_THETA)
        k = _rope(k, ROPE_THETA)
        rep = H // J
        k = jnp.repeat(k, rep, axis=2)
        v = jnp.repeat(v, rep, axis=2)
        q = q.transpose(0, 2, 1, 3)
        k = k.transpose(0, 2, 1, 3)
        v = v.transpose(0, 2, 1, 3)
        scores = jnp.einsum('bhqd,bhkd->bhqk', q, k) / jnp.sqrt(jnp.float32(hd))
        causal = jnp.tril(jnp.ones((N, N), dtype=bool))
        scores = jnp.where(causal[None, None], scores, -jnp.inf)
        weight = jax.nn.softmax(scores, axis=-1)
        out = jnp.einsum('bhqk,bhkd->bhqd', weight, v)
        out = out.transpose(0, 2, 1, 3).reshape(B, N, D)
        return out @ wo

    def _L0_attn_b_ref(X, Wq, bq, Wk, bk, Wv, bv, Wo, bo):
        import jax, jax.numpy as jnp
        import numpy as np
        N_HEADS = 16
        B, S, D = X.shape
        H = N_HEADS
        d_head = D // H
        scale = jnp.asarray(1.0 / np.sqrt(np.sqrt(d_head)), X.dtype)
        Q = (X @ Wq.T + bq).reshape(B, S, H, d_head) * scale
        K = (X @ Wk.T + bk).reshape(B, S, H, d_head) * scale
        V = (X @ Wv.T + bv).reshape(B, S, H, d_head)
        scores = jnp.einsum('bqhd,bkhd->bhqk', Q, K)
        causal = jnp.tril(jnp.ones((S, S), bool))
        scores = jnp.where(causal[None, None], scores, -jnp.inf)
        attn = jax.nn.softmax(scores.astype(jnp.float32), axis=-1).astype(X.dtype)
        out = jnp.einsum('bhqk,bkhd->bqhd', attn, V).reshape(B, S, D)
        return out @ Wo.T + bo

    def _L0_ffn_ref(h_shard, w_gate_up, w_down):
        import jax, jax.numpy as jnp
        import numpy as np
        HIDDEN = 256
        INTER = 1024
        BATCH, LOCAL_SEQ = (2, 512)
        batch, local_seq, hidden = h_shard.shape
        gate_up = jnp.einsum('bsh,oh->bso', h_shard, w_gate_up)
        gate, up = jnp.split(gate_up, 2, axis=-1)
        h = jax.nn.silu(gate) * up
        out = jnp.einsum('bsi,hi->bsh', h, w_down)
        return out
    x = L0_attn_a_x
    x = x + _L0_attn_a_ref(_layernorm(x, axis=-1), L0_attn_a_wq, L0_attn_a_wk, L0_attn_a_wv, L0_attn_a_wo)
    x = x + _L0_ffn_ref(_layernorm(x, axis=-1), L0_ffn_w_gate_up, L0_ffn_w_down)
    x = x + _L0_attn_b_ref(_layernorm(x, axis=-1), L0_attn_b_Wq, L0_attn_b_bq, L0_attn_b_Wk, L0_attn_b_bk, L0_attn_b_Wv, L0_attn_b_bv, L0_attn_b_Wo, L0_attn_b_bo)
    x = x + _L0_ffn_ref(_layernorm(x, axis=-1), L0_ffn_w_gate_up, L0_ffn_w_down)
    return x

_drawn_inputs = setup_inputs


def setup_inputs(seed=0):
    import zlib

    import numpy as np

    out = dict(_drawn_inputs(seed))
    spreads = {}
    factors = {'L0_attn_a_wq': 8.0,
     'L0_attn_a_wk': 8.0,
     'L0_attn_a_wv': 6.079,
     'L0_attn_a_wo': 6.647,
     'L0_attn_b_Wq': 8.0,
     'L0_attn_b_bq': 8.0,
     'L0_attn_b_Wk': 8.0,
     'L0_attn_b_bk': 64.0,
     'L0_attn_b_Wv': 6.473,
     'L0_attn_b_bv': 8.0,
     'L0_attn_b_Wo': 5.131,
     'L0_attn_b_bo': 12.104}
    for name, (base, spread) in spreads.items():
        noise = np.random.default_rng([zlib.crc32(name.encode()), seed]).standard_normal(out[name].shape)
        drawn = base * np.exp(spread * noise) if base else spread * noise
        out[name] = jnp.asarray(drawn.astype(out[name].dtype))
    for name, factor in factors.items():
        out[name] = (out[name] * factor).astype(out[name].dtype)
    return out
```

```python
from collections import namedtuple
from contextlib import ExitStack

import concourse.bass as bass
from concourse import mybir

F32 = mybir.dt.float32
BF16 = mybir.dt.bfloat16
ALU = mybir.AluOpType
ACT = mybir.ActivationFunctionType
AX_X = mybir.AxisListType.X
ds = bass.ds

P = 128
BATCH, SEQ, DIM = 2, 1024, 256
TILES = BATCH * SEQ // P
KC = DIM // P
CHUNK = 4
CHUNKS = TILES // CHUNK
NT = CHUNK * P
INTER = 1024
MC = INTER // P
EPS = 1e-5
NEG = -3.0e38
PARTS = 3
QB = SEQ // P
HG = 4
STEPS = 12
LEAD = 5
BEHIND = 2
MT_STEP = STEPS - LEAD + 1
MROW = 96
CHUNK_STEP = [(0, j) for j in range(4)] + [(1, j) for j in range(8)]
DIAGONAL = [s for s, (c, j) in enumerate(CHUNK_STEP) if j >= 4 * c]


class Attention:
    pass


def attention_shapes(heads, kv_heads, bias):
    a = Attention()
    d = a.d = DIM // heads
    a.heads, a.kv, a.bias = heads, kv_heads, bias
    a.kh = kv_heads * HG // heads
    a.groups = BATCH * heads // HG
    a.per_seq = heads // HG
    a.nq = heads * d
    a.nqk = (heads + kv_heads) * d
    a.nv = kv_heads * d
    a.row = PARTS * d
    a.blocks = -(-(heads + kv_heads) * a.row // P)
    a.batches = 1 if a.blocks <= 8 else 2
    
    if d == 8:
        a.q_runs = [(0, 3, 0), (0, 3, 24), (0, 3, 48)]
        a.k_runs = [(0, 3, 0), (1, 3, 24), (2, 3, 48)]
        a.scale = float(d) ** -0.5
    else:
        a.q_runs = [(0, 3, 0), (0, 2, 48), (0, 1, 80)]
        a.k_runs = [(0, 3, 0), (1, 2, 48), (2, 1, 80)]
        a.scale = float(d) ** -0.5
    a.loads = len(a.q_runs) + sum(n for _, n, _ in a.k_runs)
    return a


def max_units():
    units = []
    for i in range(QB):
        full = i // 4
        if full:
            units += [(i, 0, [h], 0, NT) for h in range(HG)]
        w = (i % 4 + 1) * P
        n = max(1, min(HG, NT // w))
        n = {4: 4, 2: 2, 1: 1}[n]
        units += [(i, full, list(range(h, h + n)), full * NT, w) for h in range(0, HG, n)]
    return units


UNITS = max_units()


def unit_runs():
    widths = [NT - max(0, j - 4 * c) * P for c, j in CHUNK_STEP]
    weights = [widths[(r - LEAD) % STEPS] for r in range(STEPS)]
    ends = [sum(weights[:r + 1]) / sum(weights) for r in range(STEPS)]
    runs = [[] for _ in range(STEPS)]
    for n in range(len(UNITS)):
        runs[min(r for r in range(STEPS) if (n + 0.5) / len(UNITS) <= ends[r] + 1e-9)].append(n)
    return runs


UNIT_RUNS = unit_runs()


def wait(eng, sem, value):
    if not isinstance(value, int) or value > 0:
        eng.wait_ge(sem, value)


def past(eng, sem, count):
    eng.wait_ge(sem, count + 1)


def open_counts(eng, *counts):
    for sem in counts:
        eng.nop().then_inc(sem, 1)


def hybrid_layer(nc, x_in, wq_a, wk_a, wv_a, wo_a, wq_b, bq_b, wk_b, bk_b, wv_b, bv_b, wo_b, bo_b,
                 w_gate_up, w_down, rope, out):
    A = attention_shapes(32, 8, False)
    B = attention_shapes(16, 16, True)
    x_rows = x_in.rearrange("b (t p) d -> p (b t) d", p=P)
    out_rows = out.rearrange("b (t p) d -> p (b t) d", p=P)
    scratch_a = nc.dram_tensor("scratch_a", (A.blocks * P, BATCH * SEQ), BF16).ap()
    scratch_m = nc.dram_tensor("scratch_m", (PARTS * HG * QB, P), BF16).ap()
    scratch_b = nc.dram_tensor("scratch_b", (B.blocks * P, BATCH * SEQ), BF16).ap()

    with ExitStack() as ctx:
        def sb(name, shape, dt=F32):
            return ctx.enter_context(nc.sbuf_tensor(name, shape, dt))

        def sems(prefix, names):
            return namedtuple(prefix, names)(*[ctx.enter_context(nc.semaphore(f"{prefix}_{n}"))
                                               for n in names.split()])

        PS = ctx.enter_context(nc.psum_tensor("PS", [P, 8, NT], F32))
        PSB = PS[:, :, :].bitcast(BF16)

        x = sb("x", [P, TILES, DIM])
        stats = sb("stats", [P, TILES, 6])
        mean_var = sb("mean_var", [P, TILES, 2])
        spread = sb("spread", [P, TILES])
        rstd = sb("rstd", [P, TILES])
        eps = sb("eps", [P, 1])
        w_qkv_a = sb("w_qkv_a", [P, KC, A.nqk + A.nv])
        w_out_a = sb("w_out_a", [P, KC, DIM])
        w_qkv_b = sb("w_qkv_b", [P, KC, 3 * DIM])
        w_out_b = sb("w_out_b", [P, KC, DIM])
        w_gu = sb("w_gu", [P, KC, 2 * INTER])
        w_dn = sb("w_dn", [P, MC, DIM])
        bias_qkv = sb("bias_qkv", [P, 3 * DIM])
        bias_out = sb("bias_out", [P, DIM])
        rope_sb = sb("rope_sb", [P, QB, 2 * A.d])
        ident = sb("ident", [P, P])
        ident_b = sb("ident_b", [P, P], BF16)
        mask_b = sb("mask_b", [P, P], BF16)
        QT = sb("QT", [P, 3, HG * SEQ], BF16)
        KT = sb("KT", [P, 3, HG * SEQ], BF16)
        v_all = sb("v_all", [P, TILES, DIM])
        v_st = sb("v_st", [P, QB, HG, 32])
        mx = sb("mx", [P, 2, QB, HG])
        neg_rest = sb("neg_rest", [P, QB, HG])
        neg_m = sb("neg_m", [P, PARTS, HG, QB], BF16)
        mT = sb("mT", [PARTS * HG * QB, P], BF16)
        o_sb = sb("o_sb", [P, NT])
        rden = sb("rden", [P, 4, HG, 1])
        attn_mem = sb("attn_mem", [P, TILES * DIM])
        attn = attn_mem[:, :].rearrange("p (t n) -> p t n", t=TILES)
        parts_T = attn_mem[:, 0:B.blocks * NT // 2].bitcast(BF16).rearrange("p (b t) -> p b t", b=B.blocks)
        work = sb("work", [P, 3 * HG * NT])
        PT = work[:, :].rearrange("p (s h q) -> p s h q", s=3, h=HG)
        hT = work[:, 0:MC * NT].rearrange("p (m t) -> p m t", m=MC)
        gate_sb = work[:, MC * NT:(MC + 2) * NT].rearrange("p (s t) -> p s t", s=2)
        raw_gu = work[:, 0:16 * DIM].rearrange("p (o n) -> p o n", o=16)
        raw_dn = work[:, 16 * DIM:16 * DIM + 2 * INTER].rearrange("p (o n) -> p o n", o=2)
        raw_b = sb("raw_b", [P, 4, KC, DIM])
        xn = sb("xn", [P, CHUNK, DIM])
        xnT = sb("xnT", [P, 2, KC, NT])
        qk = sb("qk", [P, 2, 2 * DIM])
        qk_rot = sb("qk_rot", [P, A.nqk])
        parts = sb("parts", [P, 2, B.blocks * P], BF16)

        WEIGHT_BANKS_OF = [[raw_gu[:, o + i, k * P:(k + 1) * P] for i in range(4)]
                           for k in range(KC) for o in range(0, 2 * INTER // P, 4)]
        WEIGHT_BANKS_TO = [w_gu[:, k, o * P:(o + 4) * P] for k in range(KC) for o in range(0, 2 * INTER // P, 4)]
        WEIGHT_BANKS_OF += [[raw_dn[:, o, (m + i) * P:(m + i + 1) * P] for i in range(2) for o in range(KC)]
                            for m in range(0, MC, 2)]
        WEIGHT_BANKS_TO += [w_dn[:, m:m + 2, :].rearrange("p m n -> p (m n)") for m in range(0, MC, 2)]
        WEIGHT_BANKS_OF += [[raw_b[:, n, o, k * P:(k + 1) * P] for k in range(KC) for o in range(KC)]
                            for n in range(4)]
        WEIGHT_BANKS_TO += [w_qkv_b[:, :, n * DIM:(n + 1) * DIM] for n in range(3)] + [w_out_b[:, :, :]]

        s_in = sems("start", "x wa rope wb wgu bias zero const pad ones raw_T raw_copied")
        LN = [sems(f"ln{n}", "stats aggregated spread ready") for n in range(4)]
        qkv_names = "xn_ready xt_ready xnT_ready qkv_ready qk_read v_read rotated own parts_ready pt_ready pt_copied stored"
        att_names = ("loaded m_stored m_loaded s_ready s_reduced st_ready exp_done masked pv_done v_staged o_copied "
                     "ot_ready rden_ready normed neg_step neg_ready mT_ready mT_copied")
        QKV = {L: sems(f"qkv_{L}", qkv_names) for L in "ab"}
        ATT = {L: sems(f"att_{L}", att_names) for L in "ab"}
        WO = {L: sems(f"wo_{L}", "at_ready t_ready atT_ready y_ready bias_added x_added") for L in "ab"}
        FFN = [sems(f"ffn{n}", "xn_ready xt_ready xnT_ready gu_ready silu_done h_ready y_ready x_added")
               for n in range(2)]
        s_out = sems("out", "stored")

        block = ctx.enter_context(nc.Block())

        @block.sync
        def _(sp):
            for c in range(CHUNKS):
                wait(sp, s_in.x, 16 * c)
                sp.dma_start(x[:, c * CHUNK:(c + 1) * CHUNK, :],
                             x_rows[:, c * CHUNK:(c + 1) * CHUNK, :]).then_inc(s_in.x, 16)
            sp.dma_start(w_out_a[:, :, :], wo_a.rearrange("(k p) n -> p k n", p=P)).then_inc(s_in.wa, 16)

            def store_parts(L, q, scratch):
                open_counts(sp, q.stored)
                rows = scratch.rearrange("(b p) t -> p b t", p=P)
                with sp.Fori(0, CHUNKS) as c:
                    past(sp, q.pt_copied, c * (CHUNK * L.batches) + CHUNK * L.batches)
                    sp.dma_start(rows[:, :, ds(c * NT, NT)], parts_T[:, 0:L.blocks, :]).then_inc(q.stored, 16)

            def attention(L, s, q, scratch):
                def load(g):
                    seq, j = g // L.per_seq, g % L.per_seq
                    wait(sp, s.st_ready, 2 * STEPS * (g - 2))
                    wait(sp, s.loaded, 16 * L.loads * g)
                    q_src = scratch[ds(j * (HG * L.row), HG * L.row), ds(seq * SEQ, SEQ)]
                    q_src = q_src.rearrange("(h r) t -> r h t", h=HG)
                    k_src = scratch[ds(j * (L.kh * L.row) + L.heads * L.row, L.kh * L.row), ds(seq * SEQ, SEQ)]
                    k_src = k_src.rearrange("(h r) t -> r h t", h=L.kh)
                    for part, n, row in L.q_runs:
                        dst = QT[row:row + n * L.d, ds(g % 3, 1), :].rearrange("p x (h t) -> p (x h) t", h=HG)
                        sp.dma_start(dst, q_src[part * L.d:(part + n) * L.d, :, :]).then_inc(s.loaded, 16)
                    for part, n, row in L.k_runs:
                        for r in range(n):
                            dst = KT[row + r * L.d:row + (r + 1) * L.d, ds(g % 3, 1), 0:L.kh * SEQ]
                            sp.dma_start(dst.rearrange("p x (h t) -> p (x h) t", h=L.kh),
                                         k_src[part * L.d:(part + 1) * L.d, :, :]).then_inc(s.loaded, 16)

                def load_max(g):
                    sp.wait_ge(s.mT_copied, g + 1)
                    sp.dma_start(scratch_m, mT[:, :]).then_inc(s.m_stored, 16)
                    sp.wait_ge(s.m_stored, g * 16 + 16)
                    sp.dma_start(QT[MROW:MROW + PARTS, ds(g % 3, 1), :].rearrange("p x n -> p (x n)"),
                                 scratch_m.rearrange("(r x) t -> r (x t)", r=PARTS)).then_inc(s.m_loaded, 16)

                def group(g, second=True):
                    if second:
                        load(g + 2)
                    load_max(g + 1)

                past(sp, q.stored, 16 * CHUNKS)
                sp.wait_ge(s_in.ones, 2)
                load(0)
                load(1)
                load_max(0)
                group(0)
                with sp.Fori(1, L.groups - 2) as g:
                    group(g)
                group(L.groups - 2, second=False)

            store_parts(A, QKV["a"], scratch_a)
            attention(A, ATT["a"], QKV["a"], scratch_a)
            store_parts(B, QKV["b"], scratch_b)
            attention(B, ATT["b"], QKV["b"], scratch_b)
            with sp.Fori(0, CHUNKS) as c:
                past(sp, FFN[1].x_added, c * CHUNK + CHUNK)
                sp.dma_start(out_rows[:, ds(c * CHUNK, CHUNK), :], x[:, ds(c * CHUNK, CHUNK), :])\
                    .then_inc(s_out.stored, 16)
            sp.wait_ge(s_out.stored, 16 * CHUNKS)

        @block.gpsimd
        def _(pool):
            nc.gpsimd.memset(ident[:, :], 1.0).then_inc(s_in.zero, 1)
            nc.gpsimd.memset(mask_b[:, :], 0.0).then_inc(s_in.zero, 1)
            pool.wait_ge(s_in.zero, 2)
            nc.gpsimd.affine_select(out=ident[:, :], in_=ident[:, :], compare_op=ALU.is_equal, fill=0.0, base=0,
                                    pattern=[[-1, P]], channel_multiplier=1).then_inc(s_in.zero, 1)
            nc.gpsimd.affine_select(out=mask_b[:, :], in_=mask_b[:, :], compare_op=ALU.is_ge, fill=NEG, base=0,
                                    pattern=[[-1, P]], channel_multiplier=1).then_inc(s_in.const, 1)
            pool.wait_ge(s_in.zero, 3)
            nc.gpsimd.tensor_copy(ident_b[:, :], ident[:, :]).then_inc(s_in.const, 1)
            nc.gpsimd.memset(QT[:, :, :].bitcast(F32), 0.0).then_inc(s_in.pad, 1)
            nc.gpsimd.memset(KT[:, :, :].bitcast(F32), 0.0).then_inc(s_in.pad, 1)
            nc.gpsimd.memset(v_st[:, :, :, :], 0.0).then_inc(s_in.pad, 1)
            pool.wait_ge(s_in.pad, 3)
            nc.gpsimd.memset(KT[MROW:MROW + PARTS, :, :], 1.0).then_inc(s_in.ones, 1)
            pool.wait_ge(s_in.ones, 1)
            nc.gpsimd.memset(v_st[:, :, :, A.d:A.d + 1], 1.0).then_inc(s_in.ones, 1)

            def attention(L, s):
                with pool.Fori(0, L.groups) as g:
                    for step in DIAGONAL:
                        c, j = CHUNK_STEP[step]
                        off = (j - 4 * c) * P
                        pool.wait_ge(s.exp_done, g * (2 * STEPS) + 2 * step + 2)
                        pool.nop(nofuse=True)
                        t = PT[:, step % 3, :, off:off + P]
                        nc.gpsimd.affine_select(out=t, in_=t, compare_op=ALU.is_ge, fill=0.0, base=0,
                                                pattern=[[0, HG], [1, P]], channel_multiplier=-1)\
                            .then_inc(s.masked, 1)

            attention(A, ATT["a"])
            attention(B, ATT["b"])

        @block.scalar
        def _(act):
            for dst, src in ((w_qkv_a[:, :, 0:A.nq], wq_a), (w_qkv_a[:, :, A.nq:A.nqk], wk_a),
                             (w_qkv_a[:, :, A.nqk:A.nqk + A.nv], wv_a)):
                act.dma_start(dst, src.rearrange("(k p) n -> p k n", p=P)).then_inc(s_in.wa, 16)
            act.dma_start(rope_sb[:, :, :], rope.rearrange("(t p) n -> p t n", p=P)).then_inc(s_in.rope, 16)
            act.dma_start(raw_gu, w_gate_up.rearrange("(o p) n -> p o n", p=P)).then_inc(s_in.wgu, 16)
            act.dma_start(raw_dn, w_down.rearrange("(o p) n -> p o n", p=P)).then_inc(s_in.wgu, 16)
            for n, w in enumerate((wq_b, wk_b, wv_b, wo_b)):
                act.dma_start(raw_b[:, n, :, :], w.rearrange("(o p) n -> p o n", p=P)).then_inc(s_in.wb, 16)
            for n, b in enumerate((bq_b, bk_b, bv_b)):
                act.dma_start(bias_qkv[:, n * DIM:(n + 1) * DIM], b.partition_broadcast(P)).then_inc(s_in.bias, 16)
            act.dma_start(bias_out[:, :], bo_b.partition_broadcast(P)).then_inc(s_in.bias, 16)

            def spread_of(ln):
                act.wait_ge(ln.aggregated, TILES)
                nc.scalar.activation(spread[:, :], mean_var[:, :, 1], ACT.Sqrt, bias=eps[:, 0:1]).then_inc(ln.spread, 1)

            def qkv(L, q):
                open_counts(act, q.xnT_ready, q.pt_copied)
                with act.Fori(0, CHUNKS) as c:
                    t0 = c * CHUNK

                    def copy_xT(u):
                        past(act, q.xt_ready, t0 + u + 1)
                        past(act, q.qkv_ready, t0)
                        nc.scalar.activation(xnT[:, 0, :, u * P:(u + 1) * P],
                                             PS[:, u % 2, 0:DIM].rearrange("p (k t) -> p k t", k=KC),
                                             ACT.Copy).then_inc(q.xnT_ready, 1)

                    def copy_parts(u):
                        n = L.blocks // L.batches
                        for k in range(L.batches):
                            past(act, q.pt_ready, t0 * L.batches + u * L.batches + k + 1)
                            if u == 0 and k == 0:
                                past(act, q.stored, c * 16)
                            bank = 6 + (u * L.batches + k) % 2
                            nc.scalar.activation(parts_T[:, k * n:(k + 1) * n, u * P:(u + 1) * P],
                                                 PSB[:, bank, 0:n * P].rearrange("p (b t) -> p b t", b=n),
                                                 ACT.Copy).then_inc(q.pt_copied, 1)

                    copy_xT(0)
                    copy_xT(1)
                    for u in range(CHUNK):
                        if u + 2 < CHUNK:
                            copy_xT(u + 2)
                        if u > 0:
                            copy_parts(u - 1)
                    copy_parts(CHUNK - 1)

            def transposed_weights():
                for n, dst in enumerate(WEIGHT_BANKS_TO):
                    act.wait_ge(s_in.raw_T, n + 1)
                    src = PS[:, n % 4, :]
                    if len(dst.shape) == 3:
                        src = src.rearrange("p (k c) -> p k c", k=KC)
                    nc.scalar.activation(dst, src, ACT.Copy).then_inc(s_in.raw_copied, 1)

            def attention(L, s):
                def copy_o(g, c):
                    wait(act, s.pv_done, STEPS * g + (4, STEPS)[c])
                    wait(act, s.ot_ready, 2 * g + c)
                    nc.scalar.activation(o_sb[:, :], PS[:, 6, :], ACT.Copy).then_inc(s.o_copied, 1)

                def copy_mT(g):
                    wait(act, s.mT_ready, g + 1)
                    wait(act, s.m_loaded, 16 * g)
                    nc.scalar.activation(mT[:, :], PSB[0:PARTS * HG * QB, 7, 0:P], ACT.Copy).then_inc(s.mT_copied, 1)

                def group(g, first=False, last=False):
                    for step, (c, j) in enumerate(CHUNK_STEP):
                        off = max(0, j - 4 * c) * P
                        wait(act, s.pv_done, STEPS * g + step - 2)
                        for half in range(2):
                            wait(act, s.st_ready, 2 * STEPS * g + 2 * step + half + 1)
                            nc.scalar.activation(PT[:, step % 3, 2 * half:2 * half + 2, off:NT],
                                                 PS[:, 2 * half:2 * half + 2, off:NT], ACT.Exp,
                                                 scale=L.scale).then_inc(s.exp_done, 1)
                        if step == BEHIND - 1 and not first:
                            copy_o(g - 1, 1)
                        if step == BEHIND + 3:
                            copy_o(g, 0)
                        if step == MT_STEP and not last:
                            copy_mT(g + 1)

                copy_mT(0)
                group(0, first=True)
                with act.Fori(1, L.groups - 1) as g:
                    group(g)
                group(L.groups - 1, last=True)
                copy_o(L.groups - 1, 1)

            def out_projection(s, att, L):
                act.wait_ge(att.normed, 2 * L.groups)
                with act.Fori(0, CHUNKS) as c:
                    past(act, s.t_ready, c * CHUNK)
                    for u in range(CHUNK):
                        nc.scalar.activation(xn[:, u, :], attn[:, ds(c * CHUNK + u, 1), :].rearrange("p x n -> p (x n)"),
                                             ACT.Copy).then_inc(s.at_ready, 1)

            def feed_forward(f):
                open_counts(act, f.xnT_ready)
                with act.Fori(0, CHUNKS // 2) as i:
                    for b in range(2):
                        past(act, f.xt_ready, 2 * i + (b + 1))
                        past(act, f.y_ready, i * (2 * CHUNK))
                        for k in range(KC):
                            nc.scalar.activation(xnT[:, b, k, :], PS[:, k, :], ACT.Copy).then_inc(f.xnT_ready, 1)
                        for m in range(MC):
                            n = b * MC + m
                            act.wait_ge(f.gu_ready, i * (2 * MC) + n + 1)
                            past(act, f.h_ready, i * (2 * MC) + max(0, n - 1))
                            nc.scalar.activation(gate_sb[:, m % 2, :], PS[:, 2 + 2 * (m % 2), :],
                                                 ACT.Silu).then_inc(f.silu_done, 1)

            spread_of(LN[0])
            qkv(A, QKV["a"])
            transposed_weights()
            attention(A, ATT["a"])
            out_projection(WO["a"], ATT["a"], A)
            spread_of(LN[1])
            feed_forward(FFN[0])
            spread_of(LN[2])
            qkv(B, QKV["b"])
            attention(B, ATT["b"])
            out_projection(WO["b"], ATT["b"], B)
            spread_of(LN[3])
            feed_forward(FFN[1])

        @block.vector
        def _(dve):
            nc.vector.memset(eps[:, :], EPS).then_inc(s_in.const, 1)
            nc.vector.memset(parts[:, :, :], 0.0).then_inc(s_in.const, 1)
            for t in range(TILES):
                if t % CHUNK == 0:
                    dve.wait_ge(s_in.x, 16 * (t // CHUNK + 1))
                nc.vector.bn_stats(stats[:, t, :], x[:, t, :]).then_inc(LN[0].stats, 1)

            def norm_factors(ln):
                dve.wait_ge(ln.stats, TILES)
                for t in range(TILES):
                    nc.vector.bn_aggr(mean_var[:, t, :], stats[:, t, :]).then_inc(ln.aggregated, 1)
                dve.wait_ge(ln.spread, 1)
                nc.vector.reciprocal(rstd[:, :], spread[:, :]).then_inc(ln.ready, 1)
                dve.wait_ge(ln.ready, 1)

            def x_tile(t):
                return x[:, ds(t, 1), :].rearrange("p x n -> p (x n)")

            def normed(dst, t):
                return nc.vector.tensor_scalar(dst, x_tile(t), mean_var[:, ds(t, 1), 0], rstd[:, ds(t, 1)],
                                               ALU.subtract, ALU.mult)

            def qkv(L, q):
                open_counts(dve, q.qk_read, q.v_read, q.parts_ready)
                own = 3 if L.bias else 6
                H = L.heads + L.kv
                with dve.Fori(0, CHUNKS) as c:
                    t0 = c * CHUNK

                    def norm(u):
                        past(dve, q.xt_ready, t0 + max(0, u - 1))
                        normed(xn[:, u % 2, :], t0 + u).then_inc(q.xn_ready, 1)

                    def project(u):
                        t = t0 + u
                        base = t * own
                        src = PS[:, 2 + 2 * (u % 2), 0:L.nqk]
                        r, rest = qk[:, 0, 0:L.nqk], qk[:, 1, 0:L.nqk]
                        past(dve, q.qkv_ready, t + 1)
                        if L.bias:
                            nc.vector.tensor_tensor(r, src, bias_qkv[:, 0:L.nqk], ALU.add).then_inc(q.qk_read, 1)
                            nc.vector.tensor_tensor(v_all[:, ds(t, 1), :].rearrange("p x n -> p (x n)"),
                                                    PS[:, 3 + 2 * (u % 2), 0:L.nv], bias_qkv[:, L.nqk:L.nqk + L.nv],
                                                    ALU.add).then_inc(q.v_read, 1)
                            past(dve, q.qk_read, t + 1)
                            k = 0
                        else:
                            nc.vector.tensor_copy(v_all[:, ds(t, 1), 0:L.nv].rearrange("p x n -> p (x n)"),
                                                  PS[:, 2 + 2 * (u % 2), L.nqk:L.nqk + L.nv]).then_inc(q.v_read, 1)
                            cos = rope_sb[:, ds(t % QB, 1), 0:L.d].broadcast_to([P, H, L.d])
                            nc.vector.tensor_tensor(r.rearrange("p (h d) -> p h d", d=L.d),
                                                    src.rearrange("p (h d) -> p h d", d=L.d), cos,
                                                    ALU.mult).then_inc(q.own, 1)
                            pairs = "p (h d e) -> p h d e"
                            rot = qk_rot[:, :].rearrange(pairs, h=H, e=2)
                            raw = src.rearrange(pairs, h=H, e=2)
                            sin = rope_sb[:, ds(t % QB, 1), L.d:2 * L.d].rearrange("p x (d e) -> p x d e", e=2)
                            nc.vector.tensor_tensor(rot[:, :, :, 0], raw[:, :, :, 1],
                                                    sin[:, :, :, 0].broadcast_to([P, H, L.d // 2]),
                                                    ALU.mult).then_inc(q.own, 1)
                            nc.vector.tensor_tensor(rot[:, :, :, 1], raw[:, :, :, 0],
                                                    sin[:, :, :, 1].broadcast_to([P, H, L.d // 2]),
                                                    ALU.mult).then_inc(q.qk_read, 1)
                            dve.wait_ge(q.own, base + 2)
                            past(dve, q.qk_read, t + 1)
                            nc.vector.tensor_tensor(r, r, qk_rot[:, :], ALU.add).then_inc(q.own, 1)
                            dve.wait_ge(q.own, base + 3)
                            k = 3
                        part = parts[:, u % 2, 0:H * L.row].rearrange("p (h r d) -> p h r d", r=PARTS, d=L.d)
                        r3 = r.rearrange("p (h d) -> p h d", d=L.d)
                        rest3 = rest.rearrange("p (h d) -> p h d", d=L.d)
                        past(dve, q.pt_ready, (t0 + max(0, u - 1)) * L.batches)
                        nc.vector.tensor_copy(part[:, :, 0, :], r3).then_inc(q.own, 1)
                        dve.wait_ge(q.own, base + k + 1)
                        past(dve, q.parts_ready, t)
                        nc.vector.tensor_tensor(rest3, r3, part[:, :, 0, :], ALU.subtract).then_inc(q.own, 1)
                        dve.wait_ge(q.own, base + k + 2)
                        nc.vector.tensor_copy(part[:, :, 1, :], rest3).then_inc(q.own, 1)
                        dve.wait_ge(q.own, base + k + 3)
                        nc.vector.tensor_tensor(part[:, :, 2, :], rest3, part[:, :, 1, :],
                                                ALU.subtract).then_inc(q.parts_ready, 1)

                    norm(0)
                    norm(1)
                    for u in range(CHUNK):
                        if u + 2 < CHUNK:
                            norm(u + 2)
                        project(u)

            def attention(L, s, q):
                D = L.d

                def reduce_units(g, run):
                    for n in UNIT_RUNS[run]:
                        i, which, heads, k0, w = UNITS[n]
                        wait(dve, s.s_ready, len(UNITS) * g + n + 1)
                        nc.vector.tensor_reduce(mx[:, which, i, heads[0]:heads[0] + len(heads)],
                                                PS[:, 4 + n % 2, 0:len(heads) * w].rearrange("p (h k) -> p h k", k=w),
                                                axis=AX_X, op=ALU.max).then_inc(s.s_reduced, 1)

                def negate_max(g):
                    wait(dve, s.s_reduced, len(UNITS) * (g + 1))
                    nc.vector.tensor_tensor(mx[:, 0, 4:8, :], mx[:, 0, 4:8, :], mx[:, 1, 4:8, :],
                                            ALU.max).then_inc(s.neg_step, 1)
                    m = mx[:, 0, :, :].rearrange("p i h -> p h i")
                    rest = neg_rest[:, :, :].rearrange("p i h -> p h i")
                    wait(dve, s.neg_step, 4 * g + 1)
                    wait(dve, s.mT_ready, g)
                    nc.vector.tensor_scalar(neg_m[:, 0, :, :], m, -1.0, None, ALU.mult).then_inc(s.neg_step, 1)
                    wait(dve, s.neg_step, 4 * g + 2)
                    nc.vector.scalar_tensor_tensor(out=rest, in0=m, scalar=-1.0, in1=neg_m[:, 0, :, :],
                                                   op0=ALU.mult, op1=ALU.subtract).then_inc(s.neg_step, 1)
                    wait(dve, s.neg_step, 4 * g + 3)
                    nc.vector.tensor_copy(neg_m[:, 1, :, :], rest).then_inc(s.neg_step, 1)
                    wait(dve, s.neg_step, 4 * g + 4)
                    nc.vector.tensor_tensor(neg_m[:, 2, :, :], rest, neg_m[:, 1, :, :],
                                            ALU.subtract).then_inc(s.neg_ready, 1)

                def stage_v(g):
                    wait(dve, s.pv_done, STEPS * g)
                    src = v_all[:, ds((g // L.per_seq) * QB, QB), ds((g % L.per_seq) * (L.kh * D), L.kh * D)]
                    nc.vector.tensor_copy(v_st[:, :, 0:L.kh, 0:D],
                                          src.rearrange("p t (h d) -> p t h d", d=D)).then_inc(s.v_staged, 1)

                def normalise(g, c):
                    wait(dve, s.ot_ready, 2 * g + c + 1)
                    o = PS[:, 7, :].rearrange("p (t h r) -> p t h r", t=4, h=HG)
                    wait(dve, s.normed, 2 * g + c)
                    nc.vector.reciprocal(rden[:, :, :, :], o[:, :, :, D:D + 1]).then_inc(s.rden_ready, 1)
                    wait(dve, s.rden_ready, 2 * g + c + 1)
                    dst = attn[:, ds((g // L.per_seq) * QB + 4 * c, 4), ds((g % L.per_seq) * (HG * D), HG * D)]
                    nc.vector.tensor_tensor(dst.rearrange("p t (h d) -> p t h d", d=D), o[:, :, :, 0:D],
                                            rden[:, :, :, :].broadcast_to([P, 4, HG, D]),
                                            ALU.mult).then_inc(s.normed, 1)

                def group(g, first=False, one_ahead=True, two_ahead=True):
                    for step in range(STEPS):
                        if step < STEPS - LEAD:
                            if one_ahead:
                                reduce_units(g + 1, step + LEAD)
                        elif two_ahead:
                            reduce_units(g + 2, step + LEAD - STEPS)
                        if step == BEHIND - 1:
                            stage_v(g)
                        if step == 3 and not first:
                            normalise(g - 1, 1)
                        if step == STEPS - LEAD - 1 and one_ahead:
                            negate_max(g + 1)
                        if step == 7:
                            normalise(g, 0)

                past(dve, q.v_read, TILES)
                past(dve, q.stored, 16 * CHUNKS)
                if L is B:
                    nc.vector.memset(v_st[:, :, :, D:D + 1], 1.0).then_inc(s_in.ones, 1)
                for run in range(STEPS):
                    reduce_units(0, run)
                negate_max(0)
                for run in range(LEAD):
                    reduce_units(1, run)
                group(0, first=True)
                with dve.Fori(1, L.groups - 2) as g:
                    group(g)
                group(L.groups - 2, two_ahead=False)
                group(L.groups - 1, one_ahead=False, two_ahead=False)
                normalise(L.groups - 1, 1)

            def out_projection(s, ln, bias):
                open_counts(dve, s.x_added)
                with dve.Fori(0, CHUNKS) as c:
                    t0 = c * CHUNK
                    past(dve, s.y_ready, t0)
                    for u in range(CHUNK):
                        past(dve, s.t_ready, t0 + u + 1)
                        nc.vector.tensor_copy(xnT[:, 0, :, u * P:(u + 1) * P],
                                              PS[:, u, 0:DIM].rearrange("p (k t) -> p k t", k=KC))\
                            .then_inc(s.atT_ready, 1)
                        if bias:
                            nc.vector.tensor_tensor(x_tile(t0 + u), x_tile(t0 + u), bias_out[:, :],
                                                    ALU.add).then_inc(s.bias_added, 1)
                    for u in range(CHUNK):
                        past(dve, s.y_ready, t0 + u + 1)
                        if bias:
                            dve.wait_ge(s.bias_added, t0 + u + 1)
                        nc.vector.tensor_tensor(x_tile(t0 + u), x_tile(t0 + u), PS[:, 4 + u, 0:DIM],
                                                ALU.add).then_inc(s.x_added, 1)
                    for u in range(CHUNK):
                        past(dve, s.x_added, t0 + u + 1)
                        nc.vector.bn_stats(stats[:, ds(t0 + u, 1), :].rearrange("p x n -> p (x n)"),
                                           x_tile(t0 + u)).then_inc(ln.stats, 1)

            def feed_forward(f, ln):
                open_counts(dve, f.h_ready, f.x_added)
                with dve.Fori(0, CHUNKS) as c:
                    t0 = c * CHUNK
                    past(dve, f.xt_ready, c)
                    for u in range(CHUNK):
                        normed(xn[:, u, :], t0 + u).then_inc(f.xn_ready, 1)
                    past(dve, f.y_ready, t0)
                    for m in range(MC):
                        dve.wait_ge(f.silu_done, c * MC + m + 1)
                        nc.vector.tensor_tensor(hT[:, m, :], gate_sb[:, m % 2, :], PS[:, 3 + 2 * (m % 2), :],
                                                ALU.mult).then_inc(f.h_ready, 1)
                    for u in range(CHUNK):
                        past(dve, f.y_ready, t0 + u + 1)
                        nc.vector.tensor_tensor(x_tile(t0 + u), x_tile(t0 + u), PS[:, 6 + u % 2, 0:DIM],
                                                ALU.add).then_inc(f.x_added, 1)
                        if ln is not None:
                            past(dve, f.x_added, t0 + u + 1)
                            nc.vector.bn_stats(stats[:, ds(t0 + u, 1), :].rearrange("p x n -> p (x n)"),
                                               x_tile(t0 + u)).then_inc(ln.stats, 1)

            norm_factors(LN[0])
            dve.wait_ge(s_in.rope, 16)
            qkv(A, QKV["a"])
            attention(A, ATT["a"], QKV["a"])
            out_projection(WO["a"], LN[1], False)
            norm_factors(LN[1])
            feed_forward(FFN[0], LN[2])
            norm_factors(LN[2])
            dve.wait_ge(s_in.bias, 64)
            qkv(B, QKV["b"])
            attention(B, ATT["b"], QKV["b"])
            out_projection(WO["b"], LN[3], True)
            norm_factors(LN[3])
            feed_forward(FFN[1], None)

        @block.tensor
        def _(pe):
            pe.wait_ge(s_in.const, 4)
            pe.wait_ge(s_in.wa, 16 * 4)

            def qkv(L, q, w):
                open_counts(pe, q.xt_ready, q.qkv_ready, q.pt_ready)
                with pe.Fori(0, CHUNKS) as c:
                    t0 = c * CHUNK

                    def transpose_x(u):
                        pe.wait_ge(q.xn_ready, t0 + u + 1)
                        past(pe, q.xnT_ready, t0 + max(0, u - 1))
                        nc.tensor.transpose(PS[:, u % 2, 0:P], xn[:, u % 2, 0:P], ident[:, :])
                        nc.tensor.transpose(PS[:, u % 2, P:DIM], xn[:, u % 2, P:DIM], ident[:, :])\
                            .then_inc(q.xt_ready, 1)

                    def project(u):
                        past(pe, q.xnT_ready, t0 + u + 1)
                        past(pe, q.qk_read, t0 + max(0, u - 1))
                        past(pe, q.v_read, t0 + max(0, u - 1))
                        pieces = [(0, 0, L.nqk + L.nv)] if L.nqk + L.nv <= NT else [(0, 0, L.nqk), (1, L.nqk, L.nv)]
                        for bank, n0, n in pieces:
                            for k in range(KC):
                                last = nc.tensor.matmul(PS[:, 2 + 2 * (u % 2) + bank, 0:n],
                                                        xnT[:, 0, k, u * P:(u + 1) * P], w[:, k, n0:n0 + n],
                                                        start=(k == 0), stop=(k == KC - 1))
                        last.then_inc(q.qkv_ready, 1)

                    def transpose_parts(u):
                        n = L.blocks // L.batches
                        past(pe, q.parts_ready, t0 + u + 1)
                        for k in range(L.batches):
                            b = u * L.batches + k
                            past(pe, q.pt_copied, t0 * L.batches + max(0, b - 1))
                            for i in range(n):
                                last = nc.tensor.transpose(PSB[:, 6 + b % 2, i * P:(i + 1) * P],
                                                           parts[:, u % 2, (k * n + i) * P:(k * n + i + 1) * P],
                                                           ident_b[:, :])
                            last.then_inc(q.pt_ready, 1)

                    transpose_x(0)
                    transpose_x(1)
                    for u in range(CHUNK):
                        if u + 2 < CHUNK:
                            transpose_x(u + 2)
                        project(u)
                        if u > 0:
                            transpose_parts(u - 1)
                    transpose_parts(CHUNK - 1)

            def transpose_weights():
                pe.wait_ge(s_in.wgu, 32)
                pe.wait_ge(s_in.wb, 64)
                for n, blocks in enumerate(WEIGHT_BANKS_OF):
                    wait(pe, s_in.raw_copied, n - 3)
                    for i, src in enumerate(blocks):
                        last = nc.tensor.transpose(PS[:, n % 4, i * P:(i + 1) * P], src, ident[:, :])
                    last.then_inc(s_in.raw_T, 1)

            def attention(L, s, q):
                def QTg(g):
                    return QT[:, ds(g % 3, 1), :].rearrange("p x n -> p (x n)")

                def KTg(g):
                    return KT[:, ds(g % 3, 1), :].rearrange("p x n -> p (x n)")

                def k_head(h):
                    return h if L.kh > 1 else 0

                def scores(g, units):
                    qt, kt = QTg(g), KTg(g)
                    for n in units:
                        if n == 0:
                            wait(pe, s.loaded, 16 * L.loads * (g + 1))
                        i, which, heads, k0, w = UNITS[n]
                        wait(pe, s.s_reduced, len(UNITS) * g + n - 1)
                        for x0, h in enumerate(heads):
                            dst = PS[:, 4 + n % 2, x0 * w:(x0 + 1) * w]
                            diagonal = k0 + w == (i + 1) * P
                            kcol = k_head(h) * SEQ + k0
                            last = nc.tensor.matmul(dst, qt[0:MROW, h * SEQ + i * P:h * SEQ + (i + 1) * P],
                                                    kt[0:MROW, kcol:kcol + w], start=True, stop=not diagonal)
                            if diagonal:
                                last = nc.tensor.matmul(dst[:, w - P:w], ident_b[:, :], mask_b[:, :],
                                                        start=False, stop=True)
                        last.then_inc(s.s_ready, 1)

                def scores_T(g, step, half):
                    c, j = CHUNK_STEP[step]
                    off = max(0, j - 4 * c) * P
                    qt, kt = QTg(g), KTg(g)
                    if step == 0 and half == 0:
                        wait(pe, s.m_loaded, 16 * (g + 1))
                    wait(pe, s.exp_done, 2 * STEPS * g + 2 * step + half - 1)
                    for h in (2 * half, 2 * half + 1):
                        kcol, qcol = k_head(h) * SEQ + j * P, h * SEQ + c * NT
                        last = nc.tensor.matmul(PS[:, h, off:NT], kt[:, kcol:kcol + P], qt[:, qcol + off:qcol + NT],
                                                start=True, stop=True)
                    last.then_inc(s.st_ready, 1)

                def weigh(g, step):
                    c, j = CHUNK_STEP[step]
                    off = max(0, j - 4 * c) * P
                    if step == 0:
                        wait(pe, s.v_staged, g + 1)
                    if j == 0:
                        wait(pe, s.o_copied, 2 * g + c)
                    if step in DIAGONAL:
                        wait(pe, s.masked, len(DIAGONAL) * g + DIAGONAL.index(step) + 1)
                    else:
                        wait(pe, s.exp_done, 2 * STEPS * g + 2 * step + 2)
                    for h in range(HG):
                        last = nc.tensor.matmul(PS[32 * h:32 * (h + 1), 6, off:NT], v_st[:, j, k_head(h), :],
                                                PT[:, step % 3, h, off:NT], start=(j == 0), stop=(j == 4 * c + 3))
                    last.then_inc(s.pv_done, 1)

                def transpose_o(g, c):
                    wait(pe, s.o_copied, 2 * g + c + 1)
                    if c == 0:
                        wait(pe, s.normed, 2 * g)
                    elif isinstance(g, int) and g == L.groups - 1:
                        wait(pe, s.normed, 2 * g + 1)
                    else:
                        wait(pe, s.mT_copied, g + 2)
                    for i in range(4):
                        last = nc.tensor.transpose(PS[:, 7, i * P:(i + 1) * P], o_sb[:, i * P:(i + 1) * P], ident[:, :])
                    last.then_inc(s.ot_ready, 1)

                def transpose_max(g):
                    wait(pe, s.neg_ready, g + 1)
                    wait(pe, s.normed, 2 * g - 1)
                    nc.tensor.transpose(PSB[0:PARTS * HG * QB, 7, 0:P], neg_m[:, :, :, :].rearrange("p r h i -> p (r h i)"),
                                        ident_b[:, :]).then_inc(s.mT_ready, 1)

                def group(g, first=False, one_ahead=True, two_ahead=True):
                    for step in range(STEPS):
                        ahead = g + 1 if step < STEPS - LEAD else g + 2
                        units = UNIT_RUNS[(step + LEAD) % STEPS]
                        if not (one_ahead if step < STEPS - LEAD else two_ahead):
                            units = []
                        scores_T(g, step, 0)
                        scores(ahead, units[0:1])
                        scores_T(g, step, 1)
                        scores(ahead, units[1:2])
                        if step >= BEHIND:
                            weigh(g, step - BEHIND)
                        elif not first:
                            weigh(g - 1, step - BEHIND + STEPS)
                        scores(ahead, units[2:])
                        if step == 2 and not first:
                            transpose_o(g - 1, 1)
                        if step == 6:
                            transpose_o(g, 0)
                        if step == MT_STEP and one_ahead:
                            transpose_max(g + 1)

                past(pe, q.qk_read, TILES)
                past(pe, q.v_read, TILES)
                past(pe, q.pt_copied, TILES * L.batches)
                scores(0, range(len(UNITS)))
                transpose_max(0)
                for run in range(LEAD):
                    scores(1, UNIT_RUNS[run])
                group(0, first=True)
                with pe.Fori(1, L.groups - 2) as g:
                    group(g)
                group(L.groups - 2, two_ahead=False)
                group(L.groups - 1, one_ahead=False, two_ahead=False)
                for step in range(STEPS - BEHIND, STEPS):
                    weigh(L.groups - 1, step)
                transpose_o(L.groups - 1, 1)

            def out_projection(s, w):
                open_counts(pe, s.t_ready, s.y_ready)
                with pe.Fori(0, CHUNKS) as c:
                    t0 = c * CHUNK
                    for u in range(CHUNK):
                        pe.wait_ge(s.at_ready, t0 + u + 1)
                        nc.tensor.transpose(PS[:, u, 0:P], xn[:, u, 0:P], ident[:, :])
                        nc.tensor.transpose(PS[:, u, P:DIM], xn[:, u, P:DIM], ident[:, :]).then_inc(s.t_ready, 1)
                    past(pe, s.x_added, t0)
                    for u in range(CHUNK):
                        pe.wait_ge(s.atT_ready, t0 + u + 1)
                        for k in range(KC):
                            last = nc.tensor.matmul(PS[:, 4 + u, 0:DIM], xnT[:, 0, k, u * P:(u + 1) * P], w[:, k, :],
                                                    start=(k == 0), stop=(k == KC - 1))
                        last.then_inc(s.y_ready, 1)

            def feed_forward(f):
                open_counts(pe, f.xt_ready, f.y_ready)
                with pe.Fori(0, CHUNKS // 2) as i:
                    for b in range(2):
                        c = 2 * i + b
                        past(pe, f.xnT_ready, KC * 2 * i + KC * b)
                        for u in range(CHUNK):
                            pe.wait_ge(f.xn_ready, i * (2 * CHUNK) + b * CHUNK + u + 1)
                            for k in range(KC):
                                last = nc.tensor.transpose(PS[:, k, u * P:(u + 1) * P], xn[:, u, k * P:(k + 1) * P],
                                                           ident[:, :])
                        last.then_inc(f.xt_ready, 1)
                        past(pe, f.xnT_ready, KC * 2 * i + KC * (b + 1))
                        for m in range(MC):
                            n = b * MC + m
                            past(pe, f.h_ready, i * (2 * MC) + max(0, n - 1))
                            for half in range(2):
                                for k in range(KC):
                                    col = half * INTER + m * P
                                    last = nc.tensor.matmul(PS[:, 2 + 2 * (m % 2) + half, :], w_gu[:, k, col:col + P],
                                                            xnT[:, b, k, :], start=(k == 0), stop=(k == KC - 1))
                            last.then_inc(f.gu_ready, 1)
                        for u in range(CHUNK):
                            n = b * CHUNK + u
                            past(pe, f.x_added, i * (2 * CHUNK) + max(0, n - 1))
                            for m in range(MC):
                                if u == 0:
                                    past(pe, f.h_ready, i * (2 * MC) + b * MC + m + 1)
                                last = nc.tensor.matmul(PS[:, 6 + u % 2, 0:DIM], hT[:, m, u * P:(u + 1) * P],
                                                        w_dn[:, m, :], start=(m == 0), stop=(m == MC - 1))
                            last.then_inc(f.y_ready, 1)

            qkv(A, QKV["a"], w_qkv_a)
            transpose_weights()
            attention(A, ATT["a"], QKV["a"])
            out_projection(WO["a"], w_out_a)
            feed_forward(FFN[0])
            qkv(B, QKV["b"], w_qkv_b)
            attention(B, ATT["b"], QKV["b"])
            out_projection(WO["b"], w_out_b)
            feed_forward(FFN[1])


_INS = ["L0_attn_a_x", "L0_attn_a_wq", "L0_attn_a_wk", "L0_attn_a_wv", "L0_attn_a_wo",
        "L0_attn_b_Wq", "L0_attn_b_bq", "L0_attn_b_Wk", "L0_attn_b_bk", "L0_attn_b_Wv", "L0_attn_b_bv",
        "L0_attn_b_Wo", "L0_attn_b_bo", "L0_ffn_w_gate_up", "L0_ffn_w_down"]


def _rope_table(seq, d, theta=10000.0):
    import numpy as np

    freq = (np.float32(theta) ** (-(np.arange(d // 2, dtype=np.float32) * np.float32(2.0 / d)))).astype(np.float32)
    phase = np.arange(seq, dtype=np.float32)[:, None] * freq[None, :]
    cos, sin = np.cos(phase), np.sin(phase)
    table = np.concatenate([np.repeat(cos, 2, axis=1), np.stack([-sin, sin], axis=-1).reshape(seq, d)], axis=1)
    return np.ascontiguousarray(table.astype(np.float32))


def kernel(**inputs):
    import numpy as np
    import concourse.bacc as bacc
    from concourse.bass_utils import run_bass_kernel_spmd

    nc = bacc.Bacc("TRN2", target_bir_lowering=False, num_devices=1)
    arrays = {f"in_{n}": np.ascontiguousarray(inputs[n]) for n in _INS}
    arrays["rope_table"] = _rope_table(SEQ, DIM // 32)
    args = [nc.dram_tensor(n, a.shape, mybir.dt.from_np(a.dtype), kind="ExternalInput").ap()
            for n, a in arrays.items()]
    out = nc.dram_tensor("out", (BATCH, SEQ, DIM), F32, kind="ExternalOutput").ap()
    hybrid_layer(nc, *args, out)
    return run_bass_kernel_spmd(nc, [arrays], core_ids=[0]).results[0]["out"]
```

```python
from collections import namedtuple
from contextlib import ExitStack

import concourse.bass as bass
from concourse import mybir

F32 = mybir.dt.float32
F32R = mybir.dt.float32r
BF16 = mybir.dt.bfloat16
ALU = mybir.AluOpType
ACT = mybir.ActivationFunctionType
AX_X = mybir.AxisListType.X
ds = bass.ds

P = 128
BATCH, SEQ, DIM = 2, 1024, 256
TILES = BATCH * SEQ // P
KC = DIM // P
CHUNK = 4
CHUNKS = TILES // CHUNK
NT = CHUNK * P
INTER = 1024
MC = INTER // P
SPLITS = 3 * KC * INTER // NT // CHUNKS
EPS = 1e-5
NEG = -3.0e38
PARTS = 3
QB = SEQ // P
HG = 4
STEPS = 12
LEAD = 5
BEHIND = 2
MT_STEP = STEPS - LEAD + 1
MROW = 96
CHUNK_STEP = [(0, j) for j in range(4)] + [(1, j) for j in range(8)]
DIAGONAL = [s for s, (c, j) in enumerate(CHUNK_STEP) if j >= 4 * c]


class Attention:
    pass


def attention_shapes(heads, kv_heads, bias):
    a = Attention()
    d = a.d = DIM // heads
    a.heads, a.kv, a.bias = heads, kv_heads, bias
    a.kh = kv_heads * HG // heads
    a.groups = BATCH * heads // HG
    a.per_seq = heads // HG
    a.nq = heads * d
    a.nqk = (heads + kv_heads) * d
    a.nv = kv_heads * d
    a.row = PARTS * d
    a.blocks = -(-(heads + kv_heads) * a.row // P)
    a.batches = 1 if a.blocks <= 8 else 2
    
    if d == 8:
        a.q_runs = [(0, 3, 0), (0, 3, 24), (0, 3, 48)]
        a.k_runs = [(0, 3, 0), (1, 3, 24), (2, 3, 48)]
        a.scale = float(d) ** -0.5
    else:
        a.q_runs = [(0, 3, 0), (0, 2, 48), (0, 1, 80)]
        a.k_runs = [(0, 3, 0), (1, 2, 48), (2, 1, 80)]
        a.scale = float(d) ** -0.5
    a.loads = len(a.q_runs) + sum(n for _, n, _ in a.k_runs)
    return a


def max_units():
    units = []
    for i in range(QB):
        full = i // 4
        if full:
            units += [(i, 0, [h], 0, NT) for h in range(HG)]
        w = (i % 4 + 1) * P
        n = max(1, min(HG, NT // w))
        n = {4: 4, 2: 2, 1: 1}[n]
        units += [(i, full, list(range(h, h + n)), full * NT, w) for h in range(0, HG, n)]
    return units


UNITS = max_units()


def unit_runs():
    widths = [NT - max(0, j - 4 * c) * P for c, j in CHUNK_STEP]
    weights = [widths[(r - LEAD) % STEPS] for r in range(STEPS)]
    ends = [sum(weights[:r + 1]) / sum(weights) for r in range(STEPS)]
    runs = [[] for _ in range(STEPS)]
    for n in range(len(UNITS)):
        runs[min(r for r in range(STEPS) if (n + 0.5) / len(UNITS) <= ends[r] + 1e-9)].append(n)
    return runs


UNIT_RUNS = unit_runs()


def wait(eng, sem, value):
    if not isinstance(value, int) or value > 0:
        eng.wait_ge(sem, value)


def past(eng, sem, count):
    eng.wait_ge(sem, count + 1)


def open_counts(eng, *counts):
    for sem in counts:
        eng.nop().then_inc(sem, 1)


def hybrid_layer(nc, x_in, wq_a, wk_a, wv_a, wo_a, wq_b, bq_b, wk_b, bk_b, wv_b, bv_b, wo_b, bo_b,
                 w_gate_up, w_down, rope, out):
    A = attention_shapes(32, 8, False)
    B = attention_shapes(16, 16, True)
    x_rows = x_in.rearrange("b (t p) d -> p (b t) d", p=P)
    out_rows = out.rearrange("b (t p) d -> p (b t) d", p=P)
    scratch_a = nc.dram_tensor("scratch_a", (A.blocks * P, BATCH * SEQ), BF16).ap()
    scratch_m = nc.dram_tensor("scratch_m", (PARTS * HG * QB, P), BF16).ap()
    scratch_b = nc.dram_tensor("scratch_b", (B.blocks * P, BATCH * SEQ), BF16).ap()

    with ExitStack() as ctx:
        def sb(name, shape, dt=F32):
            return ctx.enter_context(nc.sbuf_tensor(name, shape, dt))

        def sems(prefix, names):
            return namedtuple(prefix, names)(*[ctx.enter_context(nc.semaphore(f"{prefix}_{n}"))
                                               for n in names.split()])

        PS = ctx.enter_context(nc.psum_tensor("PS", [P, 8, NT], F32))
        PSB = PS[:, :, :].bitcast(BF16)

        x = sb("x", [P, TILES, DIM])
        stats = sb("stats", [P, TILES, 6])
        mean_var = sb("mean_var", [P, TILES, 2])
        spread = sb("spread", [P, TILES])
        rstd = sb("rstd", [P, TILES])
        eps = sb("eps", [P, 1])
        w_qkv_a = sb("w_qkv_a", [P, KC, A.nqk + A.nv])
        w_out_a = sb("w_out_a", [P, KC, DIM])
        w_qkv_b = sb("w_qkv_b", [P, KC, 3 * DIM])
        w_out_b = sb("w_out_b", [P, KC, DIM])
        w_ffn = sb("w_ffn", [P, (2 * KC + KC) * INTER])
        w_gu = w_ffn[:, 0:2 * KC * INTER].rearrange("p (k n) -> p k n", k=KC)
        w_dn = w_ffn[:, 2 * KC * INTER:].rearrange("p (m n) -> p m n", m=MC)
        bias_qkv = sb("bias_qkv", [P, 3 * DIM])
        bias_out = sb("bias_out", [P, DIM])
        rope_sb = sb("rope_sb", [P, QB, 2 * A.d])
        ident = sb("ident", [P, P])
        ident_b = sb("ident_b", [P, P], BF16)
        mask_b = sb("mask_b", [P, P], BF16)
        v_st = sb("v_st", [P, QB, HG, 32])
        mx = sb("mx", [P, 2, QB, HG])
        neg_rest = sb("neg_rest", [P, QB, HG])
        neg_m = sb("neg_m", [P, PARTS, HG, QB], BF16)
        mT = sb("mT", [PARTS * HG * QB, P], BF16)
        o_sb = sb("o_sb", [P, NT])
        rden = sb("rden", [P, 4, HG, 1])
        raw_b = sb("raw_b", [P, 4, KC, DIM])
        xn = sb("xn", [P, CHUNK, DIM])
        xnT = sb("xnT", [P, KC, NT])
        qk = sb("qk", [P, 2, 2 * DIM])
        qk_rest = sb("qk_rest", [P, 2, 2 * DIM])
        qk_rot = sb("qk_rot", [P, A.nqk])
        parts = sb("parts", [P, 2, B.blocks * P], BF16)

        with ExitStack() as attention_ctx:
            def att_sb(name, shape, dt=F32):
                return attention_ctx.enter_context(nc.sbuf_tensor(name, shape, dt))

            QT = att_sb("QT", [P, 3, HG * SEQ], BF16)
            KT = att_sb("KT", [P, 3, HG * SEQ], BF16)
            v_all = att_sb("v_all", [P, TILES, DIM])
            attn_mem = att_sb("attn_mem", [P, TILES * DIM])
            work = att_sb("work", [P, 3 * HG * NT])
        attn = attn_mem[:, :].rearrange("p (t n) -> p t n", t=TILES)
        parts_T = attn_mem[:, 0:B.blocks * NT // 2].bitcast(BF16).rearrange("p (b t) -> p b t", b=B.blocks)
        PT = work[:, :].rearrange("p (s h q) -> p s h q", s=3, h=HG)
        raw_gu = work[:, 0:16 * DIM].rearrange("p (o n) -> p o n", o=16)
        raw_dn = work[:, 16 * DIM:16 * DIM + 2 * INTER].rearrange("p (o n) -> p o n", o=2)
        w_split = [sb("w_high", [P, 3 * KC * INTER], F32R), sb("w_low", [P, 3 * KC * INTER], F32R)]
        xnT_split = [sb("xnT_high", [P, KC, NT], F32R), sb("xnT_low", [P, KC, NT], F32R)]
        h_split = [sb("h_high", [P, MC, NT], F32R), sb("h_low", [P, MC, NT], F32R)]
        gate_sb = sb("gate_sb", [P, 2, NT])
        h_sb = sb("h_sb", [P, 2, NT])
        w_gu_split = [w[:, 0:2 * KC * INTER].rearrange("p (k n) -> p k n", k=KC) for w in w_split]
        w_dn_split = [w[:, 2 * KC * INTER:3 * KC * INTER].rearrange("p (m n) -> p m n", m=MC) for w in w_split]

        WEIGHT_BANKS_OF = [[raw_gu[:, o + i, k * P:(k + 1) * P] for i in range(4)]
                           for k in range(KC) for o in range(0, 2 * INTER // P, 4)]
        WEIGHT_BANKS_TO = [w_gu[:, k, o * P:(o + 4) * P] for k in range(KC) for o in range(0, 2 * INTER // P, 4)]
        WEIGHT_BANKS_OF += [[raw_dn[:, o, (m + i) * P:(m + i + 1) * P] for i in range(2) for o in range(KC)]
                            for m in range(0, MC, 2)]
        WEIGHT_BANKS_TO += [w_dn[:, m:m + 2, :].rearrange("p m n -> p (m n)") for m in range(0, MC, 2)]
        WEIGHT_BANKS_OF += [[raw_b[:, n, o, k * P:(k + 1) * P] for k in range(KC) for o in range(KC)]
                            for n in range(4)]
        WEIGHT_BANKS_TO += [w_qkv_b[:, :, n * DIM:(n + 1) * DIM] for n in range(3)] + [w_out_b[:, :, :]]

        def by_head(L, buffer, u):
            return buffer[:, u % 2, 0:L.nqk].rearrange("p (h d) -> p h d", d=L.d)

        def part(L, u):
            return parts[:, u % 2, 0:(L.heads + L.kv) * L.row].rearrange("p (h r d) -> p h r d", r=PARTS, d=L.d)

        s_in = sems("start", "wa rope wb wgu bias zero const pad ones padded_again raw_T raw_copied")
        s_x = sems("x", " ".join(f"chunk{c}" for c in range(CHUNKS)))
        LN = [sems(f"ln{n}", "stats aggregated spread ready") for n in range(4)]
        qkv_names = ("xn_ready xt_ready xnT_ready qkv_ready qk_read v_read own rotated part0 rest part1 parts_ready "
                     "pt_ready pt_copied stored_even stored_odd")
        att_names = ("loaded m_stored m_loaded s_ready s_reduced st_ready exp_done masked pv_done v_staged o_copied "
                     "ot_ready rden_ready normed neg_step neg_ready mT_ready mT_copied")
        QKV = {L: sems(f"qkv_{L}", qkv_names) for L in "ab"}
        ATT = {L: sems(f"att_{L}", att_names) for L in "ab"}
        WO = {L: sems(f"wo_{L}", "split_high split_low at_ready t_ready atT_ready y_ready bias_added x_added") for L in "ab"}
        FFN = [sems(f"ffn{n}", "xn_ready xt_ready x_high x_low gu_ready silu_done h_ready h_high h_low y_ready x_added")
               for n in range(2)]
        s_out = sems("out", "stored")

        block = ctx.enter_context(nc.Block())

        @block.sync
        def _(sp):
            for c in range(CHUNKS):
                sp.dma_start(x[:, c * CHUNK:(c + 1) * CHUNK, :],
                             x_rows[:, c * CHUNK:(c + 1) * CHUNK, :]).then_inc(s_x[c], 16)
            sp.dma_start(w_out_a[:, :, :], wo_a.rearrange("(k p) n -> p k n", p=P)).then_inc(s_in.wa, 16)

            def store_parts(L, q, scratch):
                open_counts(sp, q.stored_even, q.stored_odd)
                rows = scratch.rearrange("(b p) t -> p b t", p=P)
                with sp.Fori(0, CHUNKS) as c:
                    for half, stored in enumerate((q.stored_even, q.stored_odd)):
                        past(sp, q.pt_copied, (c * CHUNK + (half + 1) * CHUNK // 2) * L.batches)
                        sp.dma_start(rows[:, :, ds(c * NT + half * NT // 2, NT // 2)],
                                     parts_T[:, 0:L.blocks, half * NT // 2:(half + 1) * NT // 2]).then_inc(stored, 16)

            def attention(L, s, q, scratch):
                def load(g):
                    seq, j = g // L.per_seq, g % L.per_seq
                    wait(sp, s.st_ready, 2 * STEPS * (g - 2))
                    wait(sp, s.loaded, 16 * L.loads * g)
                    q_src = scratch[ds(j * (HG * L.row), HG * L.row), ds(seq * SEQ, SEQ)]
                    q_src = q_src.rearrange("(h r) t -> r h t", h=HG)
                    k_src = scratch[ds(j * (L.kh * L.row) + L.heads * L.row, L.kh * L.row), ds(seq * SEQ, SEQ)]
                    k_src = k_src.rearrange("(h r) t -> r h t", h=L.kh)
                    for part, n, row in L.q_runs:
                        dst = QT[row:row + n * L.d, ds(g % 3, 1), :].rearrange("p x (h t) -> p (x h) t", h=HG)
                        sp.dma_start(dst, q_src[part * L.d:(part + n) * L.d, :, :]).then_inc(s.loaded, 16)
                    for part, n, row in L.k_runs:
                        for r in range(n):
                            dst = KT[row + r * L.d:row + (r + 1) * L.d, ds(g % 3, 1), 0:L.kh * SEQ]
                            sp.dma_start(dst.rearrange("p x (h t) -> p (x h) t", h=L.kh),
                                         k_src[part * L.d:(part + 1) * L.d, :, :]).then_inc(s.loaded, 16)

                def load_max(g):
                    sp.wait_ge(s.mT_copied, g + 1)
                    sp.dma_start(scratch_m, mT[:, :]).then_inc(s.m_stored, 16)
                    sp.wait_ge(s.m_stored, g * 16 + 16)
                    sp.dma_start(QT[MROW:MROW + PARTS, ds(g % 3, 1), :].rearrange("p x n -> p (x n)"),
                                 scratch_m.rearrange("(r x) t -> r (x t)", r=PARTS)).then_inc(s.m_loaded, 16)

                def group(g, second=True):
                    if second:
                        load(g + 2)
                    load_max(g + 1)

                past(sp, q.stored_even, 16 * CHUNKS)
                past(sp, q.stored_odd, 16 * CHUNKS)
                sp.wait_ge(s_in.ones, 2)
                if L is B:
                    sp.wait_ge(s_in.padded_again, 3)
                load(0)
                load(1)
                load_max(0)
                group(0)
                with sp.Fori(1, L.groups - 2) as g:
                    group(g)
                group(L.groups - 2, second=False)

            store_parts(A, QKV["a"], scratch_a)
            attention(A, ATT["a"], QKV["a"], scratch_a)
            store_parts(B, QKV["b"], scratch_b)
            attention(B, ATT["b"], QKV["b"], scratch_b)
            with sp.Fori(0, CHUNKS) as c:
                past(sp, FFN[1].x_added, c * CHUNK + CHUNK)
                sp.dma_start(out_rows[:, ds(c * CHUNK, CHUNK), :], x[:, ds(c * CHUNK, CHUNK), :])\
                    .then_inc(s_out.stored, 16)
            sp.wait_ge(s_out.stored, 16 * CHUNKS)

        @block.gpsimd
        def _(pool):
            nc.gpsimd.memset(ident[:, :], 1.0).then_inc(s_in.zero, 1)
            nc.gpsimd.memset(mask_b[:, :], 0.0).then_inc(s_in.zero, 1)
            pool.wait_ge(s_in.zero, 2)
            nc.gpsimd.affine_select(out=ident[:, :], in_=ident[:, :], compare_op=ALU.is_equal, fill=0.0, base=0,
                                    pattern=[[-1, P]], channel_multiplier=1).then_inc(s_in.zero, 1)
            nc.gpsimd.affine_select(out=mask_b[:, :], in_=mask_b[:, :], compare_op=ALU.is_ge, fill=NEG, base=0,
                                    pattern=[[-1, P]], channel_multiplier=1).then_inc(s_in.const, 1)
            pool.wait_ge(s_in.zero, 3)
            nc.gpsimd.tensor_copy(ident_b[:, :], ident[:, :]).then_inc(s_in.const, 1)
            nc.gpsimd.memset(QT[:, :, :].bitcast(F32), 0.0).then_inc(s_in.pad, 1)
            nc.gpsimd.memset(KT[:, :, :].bitcast(F32), 0.0).then_inc(s_in.pad, 1)
            nc.gpsimd.memset(v_st[:, :, :, :], 0.0).then_inc(s_in.pad, 1)
            pool.wait_ge(s_in.pad, 3)
            nc.gpsimd.memset(KT[MROW:MROW + PARTS, :, :], 1.0).then_inc(s_in.ones, 1)
            pool.wait_ge(s_in.ones, 1)
            nc.gpsimd.memset(v_st[:, :, :, A.d:A.d + 1], 1.0).then_inc(s_in.ones, 1)

            def attention(L, s):
                with pool.Fori(0, L.groups) as g:
                    for step in DIAGONAL:
                        c, j = CHUNK_STEP[step]
                        off = (j - 4 * c) * P
                        pool.wait_ge(s.exp_done, g * (2 * STEPS) + 2 * step + 2)
                        pool.nop(nofuse=True)
                        t = PT[:, step % 3, :, off:off + P]
                        nc.gpsimd.affine_select(out=t, in_=t, compare_op=ALU.is_ge, fill=0.0, base=0,
                                                pattern=[[0, HG], [1, P]], channel_multiplier=-1)\
                            .then_inc(s.masked, 1)

            attention(A, ATT["a"])
            past(pool, FFN[0].x_added, TILES)
            nc.gpsimd.memset(QT[:, :, :].bitcast(F32), 0.0).then_inc(s_in.padded_again, 1)
            nc.gpsimd.memset(KT[:, :, :].bitcast(F32), 0.0).then_inc(s_in.padded_again, 1)
            pool.wait_ge(s_in.padded_again, 2)
            nc.gpsimd.memset(KT[MROW:MROW + PARTS, :, :], 1.0).then_inc(s_in.padded_again, 1)
            attention(B, ATT["b"])

        @block.scalar
        def _(act):
            for dst, src in ((w_qkv_a[:, :, 0:A.nq], wq_a), (w_qkv_a[:, :, A.nq:A.nqk], wk_a),
                             (w_qkv_a[:, :, A.nqk:A.nqk + A.nv], wv_a)):
                act.dma_start(dst, src.rearrange("(k p) n -> p k n", p=P)).then_inc(s_in.wa, 16)
            act.dma_start(rope_sb[:, :, :], rope.rearrange("(t p) n -> p t n", p=P)).then_inc(s_in.rope, 16)
            for c in range(CHUNKS):
                act.wait_ge(s_x[c], 16)
            act.dma_start(raw_gu, w_gate_up.rearrange("(o p) n -> p o n", p=P)).then_inc(s_in.wgu, 16)
            act.dma_start(raw_dn, w_down.rearrange("(o p) n -> p o n", p=P)).then_inc(s_in.wgu, 16)
            for n, w in enumerate((wq_b, wk_b, wv_b, wo_b)):
                act.dma_start(raw_b[:, n, :, :], w.rearrange("(o p) n -> p o n", p=P)).then_inc(s_in.wb, 16)
            for n, b in enumerate((bq_b, bk_b, bv_b)):
                act.dma_start(bias_qkv[:, n * DIM:(n + 1) * DIM], b.partition_broadcast(P)).then_inc(s_in.bias, 16)
            act.dma_start(bias_out[:, :], bo_b.partition_broadcast(P)).then_inc(s_in.bias, 16)

            def spread_of(ln):
                act.wait_ge(ln.aggregated, TILES)
                nc.scalar.activation(spread[:, :], mean_var[:, :, 1], ACT.Sqrt, bias=eps[:, 0:1]).then_inc(ln.spread, 1)

            def qkv(L, q):
                open_counts(act, q.xnT_ready, q.pt_copied)

                def copy_xT(t0, u):
                    past(act, q.xt_ready, t0 + u + 1)
                    slot = u % CHUNK
                    nc.scalar.activation(xnT[:, :, slot * P:(slot + 1) * P],
                                         PS[:, u % 2, 0:DIM].rearrange("p (k t) -> p k t", k=KC),
                                         ACT.Copy).then_inc(q.xnT_ready, 1)

                def part0(t0, u):
                    past(act, q.rotated, t0 + u + 1)
                    past(act, q.pt_ready, (t0 + max(0, u - 1)) * L.batches)
                    nc.scalar.activation(part(L, u)[:, :, 0, :], by_head(L, qk, u), ACT.Copy).then_inc(q.part0, 1)

                def part1(t0, u):
                    act.wait_ge(q.rest, t0 + u + 1)
                    nc.scalar.activation(part(L, u)[:, :, 1, :], by_head(L, qk_rest, u), ACT.Copy).then_inc(q.part1, 1)

                def copy_parts(t0, u):
                    n = L.blocks // L.batches
                    for k in range(L.batches):
                        past(act, q.pt_ready, (t0 + u) * L.batches + k + 1)
                        if u % 2 == 0 and k == 0:
                            past(act, (q.stored_even, q.stored_odd)[u // 2], t0 // CHUNK * 16)
                        bank = 6 + (u * L.batches + k) % 2
                        nc.scalar.activation(parts_T[:, k * n:(k + 1) * n, u * P:(u + 1) * P],
                                             PSB[:, bank, 0:n * P].rearrange("p (b t) -> p b t", b=n),
                                             ACT.Copy).then_inc(q.pt_copied, 1)

                def chunk(t0, last=False):
                    for u in range(CHUNK):
                        if not last or u + 1 < CHUNK:
                            part0(t0, u + 1)
                            part1(t0, u + 1)
                        if not last:
                            copy_xT(t0, u + 4)
                        copy_parts(t0, u)

                for u in range(4):
                    copy_xT(0, u)
                part0(0, 0)
                part1(0, 0)
                with act.Fori(0, CHUNKS - 1) as c:
                    chunk(c * CHUNK)
                chunk((CHUNKS - 1) * CHUNK, last=True)

            def transposed_weights():
                for n, dst in enumerate(WEIGHT_BANKS_TO):
                    act.wait_ge(s_in.raw_T, n + 1)
                    src = PS[:, n % 4, :]
                    if len(dst.shape) == 3:
                        src = src.rearrange("p (k c) -> p k c", k=KC)
                    nc.scalar.activation(dst, src, ACT.Copy).then_inc(s_in.raw_copied, 1)

            def attention(L, s):
                def copy_o(g, c):
                    wait(act, s.pv_done, STEPS * g + (4, STEPS)[c])
                    wait(act, s.ot_ready, 2 * g + c)
                    nc.scalar.activation(o_sb[:, :], PS[:, 6, :], ACT.Copy).then_inc(s.o_copied, 1)

                def copy_mT(g):
                    wait(act, s.mT_ready, g + 1)
                    wait(act, s.m_loaded, 16 * g)
                    nc.scalar.activation(mT[:, :], PSB[0:PARTS * HG * QB, 7, 0:P], ACT.Copy).then_inc(s.mT_copied, 1)

                def group(g, first=False, last=False):
                    for step, (c, j) in enumerate(CHUNK_STEP):
                        off = max(0, j - 4 * c) * P
                        wait(act, s.pv_done, STEPS * g + step - 2)
                        for half in range(2):
                            wait(act, s.st_ready, 2 * STEPS * g + 2 * step + half + 1)
                            nc.scalar.activation(PT[:, step % 3, 2 * half:2 * half + 2, off:NT],
                                                 PS[:, 2 * half:2 * half + 2, off:NT], ACT.Exp,
                                                 scale=L.scale).then_inc(s.exp_done, 1)
                        if step == BEHIND - 1 and not first:
                            copy_o(g - 1, 1)
                        if step == BEHIND + 3:
                            copy_o(g, 0)
                        if step == MT_STEP and not last:
                            copy_mT(g + 1)

                copy_mT(0)
                group(0, first=True)
                with act.Fori(1, L.groups - 1) as g:
                    group(g)
                group(L.groups - 1, last=True)
                copy_o(L.groups - 1, 1)

            def out_projection(s, att, L):
                act.wait_ge(att.normed, 2 * L.groups)
                with act.Fori(0, CHUNKS) as c:
                    past(act, s.t_ready, c * CHUNK)
                    for u in range(CHUNK):
                        nc.scalar.activation(xn[:, u, :], attn[:, ds(c * CHUNK + u, 1), :].rearrange("p x n -> p (x n)"),
                                             ACT.Copy).then_inc(s.at_ready, 1)
                    for i in range(SPLITS):
                        piece = ds(c * (SPLITS * NT) + i * NT, NT)
                        nc.scalar.activation(w_split[0][:, piece], w_ffn[:, piece], ACT.Copy).then_inc(s.split_high, 1)

            def feed_forward(f):
                open_counts(act, f.x_high)

                def x_high(c):
                    for k in range(KC):
                        act.wait_ge(f.xt_ready, KC * c + k + 1)
                        nc.scalar.activation(xnT_split[0][:, k, :], PS[:, k, :], ACT.Copy).then_inc(f.x_high, 1)

                def h_high(c, m):
                    past(act, f.h_ready, MC * c + m + 1)
                    nc.scalar.activation(h_split[0][:, m, :], h_sb[:, m % 2, :], ACT.Copy).then_inc(f.h_high, 1)

                def chunk(c, last=False):
                    for m in range(MC):
                        act.wait_ge(f.gu_ready, MC * c + m + 1)
                        past(act, f.h_ready, MC * c + max(0, m - 1))
                        nc.scalar.activation(gate_sb[:, m % 2, :], PS[:, 2 + 2 * (m % 2), :],
                                             ACT.Silu).then_inc(f.silu_done, 1)
                        if m > 0:
                            h_high(c, m - 1)
                    h_high(c, MC - 1)
                    if not last:
                        x_high(c + 1)

                x_high(0)
                with act.Fori(0, CHUNKS - 1) as c:
                    chunk(c)
                chunk(CHUNKS - 1, last=True)

            spread_of(LN[0])
            qkv(A, QKV["a"])
            transposed_weights()
            attention(A, ATT["a"])
            out_projection(WO["a"], ATT["a"], A)
            spread_of(LN[1])
            feed_forward(FFN[0])
            spread_of(LN[2])
            qkv(B, QKV["b"])
            attention(B, ATT["b"])
            out_projection(WO["b"], ATT["b"], B)
            spread_of(LN[3])
            feed_forward(FFN[1])

        @block.vector
        def _(dve):
            nc.vector.memset(eps[:, :], EPS).then_inc(s_in.const, 1)
            nc.vector.memset(parts[:, :, :], 0.0).then_inc(s_in.const, 1)
            for t in range(TILES):
                if t % CHUNK == 0:
                    dve.wait_ge(s_x[t // CHUNK], 16)
                nc.vector.bn_stats(stats[:, t, :], x[:, t, :]).then_inc(LN[0].stats, 1)

            def norm_factors(ln):
                dve.wait_ge(ln.stats, TILES)
                for t in range(TILES):
                    nc.vector.bn_aggr(mean_var[:, t, :], stats[:, t, :]).then_inc(ln.aggregated, 1)
                dve.wait_ge(ln.spread, 1)
                nc.vector.reciprocal(rstd[:, :], spread[:, :]).then_inc(ln.ready, 1)
                dve.wait_ge(ln.ready, 1)

            def x_tile(t):
                return x[:, ds(t, 1), :].rearrange("p x n -> p (x n)")

            def normed(dst, t):
                return nc.vector.tensor_scalar(dst, x_tile(t), mean_var[:, ds(t, 1), 0], rstd[:, ds(t, 1)],
                                               ALU.subtract, ALU.mult)

            def qkv(L, q):
                open_counts(dve, q.qk_read, q.v_read, q.rotated, q.parts_ready)
                H = L.heads + L.kv

                def norm(t0, u):
                    past(dve, q.xt_ready, t0 + max(0, u - CHUNK + 1))
                    normed(xn[:, u % CHUNK, :], t0 + u).then_inc(q.xn_ready, 1)

                def project(t0, u):
                    t = t0 + u
                    src = PS[:, 2 + 2 * (u % 2), 0:L.nqk]
                    r = qk[:, u % 2, 0:L.nqk]
                    past(dve, q.qkv_ready, t + 1)
                    past(dve, q.parts_ready, t0 + max(0, u - 1))
                    if L.bias:
                        nc.vector.tensor_tensor(r, src, bias_qkv[:, 0:L.nqk], ALU.add).then_inc(q.rotated, 1)
                        nc.vector.tensor_tensor(v_all[:, ds(t, 1), :].rearrange("p x n -> p (x n)"),
                                                PS[:, 3 + 2 * (u % 2), 0:L.nv], bias_qkv[:, L.nqk:L.nqk + L.nv],
                                                ALU.add).then_inc(q.v_read, 1)
                        return
                    cos = rope_sb[:, ds(t % QB, 1), 0:L.d].broadcast_to([P, H, L.d])
                    nc.vector.tensor_tensor(r.rearrange("p (h d) -> p h d", d=L.d),
                                            src.rearrange("p (h d) -> p h d", d=L.d), cos,
                                            ALU.mult).then_inc(q.own, 1)
                    past(dve, q.rotated, t)
                    pairs = "p (h d e) -> p h d e"
                    rot = qk_rot[:, :].rearrange(pairs, h=H, e=2)
                    raw = src.rearrange(pairs, h=H, e=2)
                    sin = rope_sb[:, ds(t % QB, 1), L.d:2 * L.d].rearrange("p x (d e) -> p x d e", e=2)
                    nc.vector.tensor_tensor(rot[:, :, :, 0], raw[:, :, :, 1],
                                            sin[:, :, :, 0].broadcast_to([P, H, L.d // 2]),
                                            ALU.mult).then_inc(q.own, 1)
                    nc.vector.tensor_tensor(rot[:, :, :, 1], raw[:, :, :, 0],
                                            sin[:, :, :, 1].broadcast_to([P, H, L.d // 2]),
                                            ALU.mult).then_inc(q.qk_read, 1)
                    nc.vector.tensor_copy(v_all[:, ds(t, 1), 0:L.nv].rearrange("p x n -> p (x n)"),
                                          PS[:, 2 + 2 * (u % 2), L.nqk:L.nqk + L.nv]).then_inc(q.v_read, 1)
                    dve.wait_ge(q.own, t * 2 + 2)
                    past(dve, q.qk_read, t + 1)
                    nc.vector.tensor_tensor(r, r, qk_rot[:, :], ALU.add).then_inc(q.rotated, 1)

                def rest(t0, u):
                    dve.wait_ge(q.part0, t0 + u + 1)
                    nc.vector.tensor_tensor(by_head(L, qk_rest, u), by_head(L, qk, u), part(L, u)[:, :, 0, :],
                                            ALU.subtract).then_inc(q.rest, 1)

                def part2(t0, u):
                    dve.wait_ge(q.part1, t0 + u + 1)
                    nc.vector.tensor_tensor(part(L, u)[:, :, 2, :], by_head(L, qk_rest, u), part(L, u)[:, :, 1, :],
                                            ALU.subtract).then_inc(q.parts_ready, 1)

                def chunk(t0, last=False):
                    for u in range(CHUNK):
                        more = not last or u + 1 < CHUNK
                        if more:
                            project(t0, u + 1)
                        part2(t0, u)
                        if not last:
                            norm(t0, u + 4)
                        if more:
                            rest(t0, u + 1)

                for u in range(CHUNK):
                    norm(0, u)
                project(0, 0)
                rest(0, 0)
                with dve.Fori(0, CHUNKS - 1) as c:
                    chunk(c * CHUNK)
                chunk((CHUNKS - 1) * CHUNK, last=True)

            def attention(L, s, q):
                D = L.d

                def reduce_units(g, run):
                    for n in UNIT_RUNS[run]:
                        i, which, heads, k0, w = UNITS[n]
                        wait(dve, s.s_ready, len(UNITS) * g + n + 1)
                        nc.vector.tensor_reduce(mx[:, which, i, heads[0]:heads[0] + len(heads)],
                                                PS[:, 4 + n % 2, 0:len(heads) * w].rearrange("p (h k) -> p h k", k=w),
                                                axis=AX_X, op=ALU.max).then_inc(s.s_reduced, 1)

                def negate_max(g):
                    wait(dve, s.s_reduced, len(UNITS) * (g + 1))
                    nc.vector.tensor_tensor(mx[:, 0, 4:8, :], mx[:, 0, 4:8, :], mx[:, 1, 4:8, :],
                                            ALU.max).then_inc(s.neg_step, 1)
                    m = mx[:, 0, :, :].rearrange("p i h -> p h i")
                    rest = neg_rest[:, :, :].rearrange("p i h -> p h i")
                    wait(dve, s.neg_step, 4 * g + 1)
                    wait(dve, s.mT_ready, g)
                    nc.vector.tensor_scalar(neg_m[:, 0, :, :], m, -1.0, None, ALU.mult).then_inc(s.neg_step, 1)
                    wait(dve, s.neg_step, 4 * g + 2)
                    nc.vector.scalar_tensor_tensor(out=rest, in0=m, scalar=-1.0, in1=neg_m[:, 0, :, :],
                                                   op0=ALU.mult, op1=ALU.subtract).then_inc(s.neg_step, 1)
                    wait(dve, s.neg_step, 4 * g + 3)
                    nc.vector.tensor_copy(neg_m[:, 1, :, :], rest).then_inc(s.neg_step, 1)
                    wait(dve, s.neg_step, 4 * g + 4)
                    nc.vector.tensor_tensor(neg_m[:, 2, :, :], rest, neg_m[:, 1, :, :],
                                            ALU.subtract).then_inc(s.neg_ready, 1)

                def stage_v(g):
                    wait(dve, s.pv_done, STEPS * g)
                    src = v_all[:, ds((g // L.per_seq) * QB, QB), ds((g % L.per_seq) * (L.kh * D), L.kh * D)]
                    nc.vector.tensor_copy(v_st[:, :, 0:L.kh, 0:D],
                                          src.rearrange("p t (h d) -> p t h d", d=D)).then_inc(s.v_staged, 1)

                def normalise(g, c):
                    wait(dve, s.ot_ready, 2 * g + c + 1)
                    o = PS[:, 7, :].rearrange("p (t h r) -> p t h r", t=4, h=HG)
                    wait(dve, s.normed, 2 * g + c)
                    nc.vector.reciprocal(rden[:, :, :, :], o[:, :, :, D:D + 1]).then_inc(s.rden_ready, 1)
                    wait(dve, s.rden_ready, 2 * g + c + 1)
                    dst = attn[:, ds((g // L.per_seq) * QB + 4 * c, 4), ds((g % L.per_seq) * (HG * D), HG * D)]
                    nc.vector.tensor_tensor(dst.rearrange("p t (h d) -> p t h d", d=D), o[:, :, :, 0:D],
                                            rden[:, :, :, :].broadcast_to([P, 4, HG, D]),
                                            ALU.mult).then_inc(s.normed, 1)

                def group(g, first=False, one_ahead=True, two_ahead=True):
                    for step in range(STEPS):
                        if step < STEPS - LEAD:
                            if one_ahead:
                                reduce_units(g + 1, step + LEAD)
                        elif two_ahead:
                            reduce_units(g + 2, step + LEAD - STEPS)
                        if step == BEHIND - 1:
                            stage_v(g)
                        if step == 3 and not first:
                            normalise(g - 1, 1)
                        if step == STEPS - LEAD - 1 and one_ahead:
                            negate_max(g + 1)
                        if step == 7:
                            normalise(g, 0)

                past(dve, q.v_read, TILES)
                past(dve, q.stored_even, 16 * CHUNKS)
                past(dve, q.stored_odd, 16 * CHUNKS)
                if L is B:
                    nc.vector.memset(v_st[:, :, :, D:D + 1], 1.0).then_inc(s_in.ones, 1)
                for run in range(STEPS):
                    reduce_units(0, run)
                negate_max(0)
                for run in range(LEAD):
                    reduce_units(1, run)
                group(0, first=True)
                with dve.Fori(1, L.groups - 2) as g:
                    group(g)
                group(L.groups - 2, two_ahead=False)
                group(L.groups - 1, one_ahead=False, two_ahead=False)
                normalise(L.groups - 1, 1)

            def out_projection(s, ln, bias):
                open_counts(dve, s.x_added)
                with dve.Fori(0, CHUNKS) as c:
                    t0 = c * CHUNK
                    past(dve, s.y_ready, t0)
                    for u in range(CHUNK):
                        past(dve, s.t_ready, t0 + u + 1)
                        nc.vector.tensor_copy(xnT[:, :, u * P:(u + 1) * P],
                                              PS[:, u, 0:DIM].rearrange("p (k t) -> p k t", k=KC))\
                            .then_inc(s.atT_ready, 1)
                        if bias:
                            nc.vector.tensor_tensor(x_tile(t0 + u), x_tile(t0 + u), bias_out[:, :],
                                                    ALU.add).then_inc(s.bias_added, 1)
                    for i in range(SPLITS):
                        dve.wait_ge(s.split_high, c * SPLITS + i + 1)
                        piece = ds(c * (SPLITS * NT) + i * NT, NT)
                        nc.vector.tensor_tensor(w_split[1][:, piece], w_ffn[:, piece], w_split[0][:, piece].bitcast(F32),
                                                ALU.subtract).then_inc(s.split_low, 1)
                    for u in range(CHUNK):
                        past(dve, s.y_ready, t0 + u + 1)
                        if bias:
                            dve.wait_ge(s.bias_added, t0 + u + 1)
                        nc.vector.tensor_tensor(x_tile(t0 + u), x_tile(t0 + u), PS[:, 4 + u, 0:DIM],
                                                ALU.add).then_inc(s.x_added, 1)
                    for u in range(CHUNK):
                        past(dve, s.x_added, t0 + u + 1)
                        nc.vector.bn_stats(stats[:, ds(t0 + u, 1), :].rearrange("p x n -> p (x n)"),
                                           x_tile(t0 + u)).then_inc(ln.stats, 1)

            def feed_forward(f, ln):
                open_counts(dve, f.h_ready, f.h_low, f.x_low, f.x_added)

                def norm(c, u):
                    wait(dve, f.xt_ready, KC * c)
                    normed(xn[:, u, :], c * CHUNK + u).then_inc(f.xn_ready, 1)

                def x_low(c):
                    for k in range(KC):
                        past(dve, f.x_high, KC * c + k + 1)
                        nc.vector.tensor_tensor(xnT_split[1][:, k, :], PS[:, k, :], xnT_split[0][:, k, :].bitcast(F32),
                                                ALU.subtract).then_inc(f.x_low, 1)

                def h_low(c, m):
                    dve.wait_ge(f.h_high, MC * c + m + 1)
                    nc.vector.tensor_tensor(h_split[1][:, m, :], h_sb[:, m % 2, :], h_split[0][:, m, :].bitcast(F32),
                                            ALU.subtract).then_inc(f.h_low, 1)

                def chunk(c, last=False):
                    for m in range(MC):
                        dve.wait_ge(f.silu_done, MC * c + m + 1)
                        past(dve, f.h_low, MC * c + max(0, m - 1))
                        nc.vector.tensor_tensor(h_sb[:, m % 2, :], gate_sb[:, m % 2, :], PS[:, 3 + 2 * (m % 2), :],
                                                ALU.mult).then_inc(f.h_ready, 1)
                        if m > 0:
                            h_low(c, m - 1)
                        if 0 < m <= CHUNK and not last:
                            norm(c + 1, m - 1)
                    h_low(c, MC - 1)
                    if not last:
                        x_low(c + 1)
                    for u in range(CHUNK):
                        t = c * CHUNK + u
                        past(dve, f.y_ready, t + 1)
                        nc.vector.tensor_tensor(x_tile(t), x_tile(t), PS[:, 6 + u % 2, 0:DIM],
                                                ALU.add).then_inc(f.x_added, 1)
                        if ln is not None:
                            past(dve, f.x_added, t + 1)
                            nc.vector.bn_stats(stats[:, ds(t, 1), :].rearrange("p x n -> p (x n)"),
                                               x_tile(t)).then_inc(ln.stats, 1)

                for u in range(CHUNK):
                    norm(0, u)
                x_low(0)
                with dve.Fori(0, CHUNKS - 1) as c:
                    chunk(c)
                chunk(CHUNKS - 1, last=True)

            norm_factors(LN[0])
            dve.wait_ge(s_in.rope, 16)
            qkv(A, QKV["a"])
            attention(A, ATT["a"], QKV["a"])
            out_projection(WO["a"], LN[1], False)
            norm_factors(LN[1])
            feed_forward(FFN[0], LN[2])
            norm_factors(LN[2])
            dve.wait_ge(s_in.bias, 64)
            qkv(B, QKV["b"])
            attention(B, ATT["b"], QKV["b"])
            out_projection(WO["b"], LN[3], True)
            norm_factors(LN[3])
            feed_forward(FFN[1], None)

        @block.tensor
        def _(pe):
            pe.wait_ge(s_in.const, 4)
            pe.wait_ge(s_in.wa, 16 * 4)

            def qkv(L, q, w):
                open_counts(pe, q.xt_ready, q.qkv_ready, q.pt_ready)

                def transpose_x(t0, u):
                    pe.wait_ge(q.xn_ready, t0 + u + 1)
                    past(pe, q.xnT_ready, t0 + max(0, u - 1))
                    for k in range(KC):
                        last = nc.tensor.transpose(PS[:, u % 2, k * P:(k + 1) * P],
                                                   xn[:, u % CHUNK, k * P:(k + 1) * P], ident[:, :])
                    last.then_inc(q.xt_ready, 1)

                def project(t0, u):
                    past(pe, q.xnT_ready, t0 + u + 1)
                    past(pe, q.rotated if L.bias else q.qk_read, t0 + max(0, u - 1))
                    past(pe, q.v_read, t0 + max(0, u - 1))
                    pieces = [(0, 0, L.nqk), (1, L.nqk, L.nv)] if L.bias else [(0, 0, L.nqk + L.nv)]
                    slot = u % CHUNK
                    for bank, n0, n in pieces:
                        for k in range(KC):
                            last = nc.tensor.matmul(PS[:, 2 + 2 * (u % 2) + bank, 0:n],
                                                    xnT[:, k, slot * P:(slot + 1) * P], w[:, k, n0:n0 + n],
                                                    start=(k == 0), stop=(k == KC - 1))
                    last.then_inc(q.qkv_ready, 1)

                def transpose_parts(t0, u):
                    n = L.blocks // L.batches
                    past(pe, q.parts_ready, t0 + u + 1)
                    for k in range(L.batches):
                        b = u * L.batches + k
                        past(pe, q.pt_copied, t0 * L.batches + max(0, b - 1))
                        for i in range(n):
                            last = nc.tensor.transpose(PSB[:, 6 + b % 2, i * P:(i + 1) * P],
                                                       parts[:, u % 2, (k * n + i) * P:(k * n + i + 1) * P],
                                                       ident_b[:, :])
                        last.then_inc(q.pt_ready, 1)

                def chunk(t0, last=False):
                    for u in range(CHUNK):
                        if not last or u + 2 < CHUNK:
                            project(t0, u + 2)
                        if not last:
                            transpose_x(t0, u + 4)
                        transpose_parts(t0, u)

                for u in range(2):
                    transpose_x(0, 2 * u)
                    transpose_x(0, 2 * u + 1)
                    project(0, u)
                with pe.Fori(0, CHUNKS - 1) as c:
                    chunk(c * CHUNK)
                chunk((CHUNKS - 1) * CHUNK, last=True)

            def transpose_weights():
                pe.wait_ge(s_in.wgu, 32)
                pe.wait_ge(s_in.wb, 64)
                for n, blocks in enumerate(WEIGHT_BANKS_OF):
                    wait(pe, s_in.raw_copied, n - 3)
                    for i, src in enumerate(blocks):
                        last = nc.tensor.transpose(PS[:, n % 4, i * P:(i + 1) * P], src, ident[:, :])
                    last.then_inc(s_in.raw_T, 1)

            def attention(L, s, q):
                def QTg(g):
                    return QT[:, ds(g % 3, 1), :].rearrange("p x n -> p (x n)")

                def KTg(g):
                    return KT[:, ds(g % 3, 1), :].rearrange("p x n -> p (x n)")

                def k_head(h):
                    return h if L.kh > 1 else 0

                def scores(g, units):
                    qt, kt = QTg(g), KTg(g)
                    for n in units:
                        if n == 0:
                            wait(pe, s.loaded, 16 * L.loads * (g + 1))
                        i, which, heads, k0, w = UNITS[n]
                        wait(pe, s.s_reduced, len(UNITS) * g + n - 1)
                        for x0, h in enumerate(heads):
                            dst = PS[:, 4 + n % 2, x0 * w:(x0 + 1) * w]
                            diagonal = k0 + w == (i + 1) * P
                            kcol = k_head(h) * SEQ + k0
                            last = nc.tensor.matmul(dst, qt[0:MROW, h * SEQ + i * P:h * SEQ + (i + 1) * P],
                                                    kt[0:MROW, kcol:kcol + w], start=True, stop=not diagonal)
                            if diagonal:
                                last = nc.tensor.matmul(dst[:, w - P:w], ident_b[:, :], mask_b[:, :],
                                                        start=False, stop=True)
                        last.then_inc(s.s_ready, 1)

                def scores_T(g, step, half):
                    c, j = CHUNK_STEP[step]
                    off = max(0, j - 4 * c) * P
                    qt, kt = QTg(g), KTg(g)
                    if step == 0 and half == 0:
                        wait(pe, s.m_loaded, 16 * (g + 1))
                    wait(pe, s.exp_done, 2 * STEPS * g + 2 * step + half - 1)
                    for h in (2 * half, 2 * half + 1):
                        kcol, qcol = k_head(h) * SEQ + j * P, h * SEQ + c * NT
                        last = nc.tensor.matmul(PS[:, h, off:NT], kt[:, kcol:kcol + P], qt[:, qcol + off:qcol + NT],
                                                start=True, stop=True)
                    last.then_inc(s.st_ready, 1)

                def weigh(g, step):
                    c, j = CHUNK_STEP[step]
                    off = max(0, j - 4 * c) * P
                    if step == 0:
                        wait(pe, s.v_staged, g + 1)
                    if j == 0:
                        wait(pe, s.o_copied, 2 * g + c)
                    if step in DIAGONAL:
                        wait(pe, s.masked, len(DIAGONAL) * g + DIAGONAL.index(step) + 1)
                    else:
                        wait(pe, s.exp_done, 2 * STEPS * g + 2 * step + 2)
                    for h in range(HG):
                        last = nc.tensor.matmul(PS[32 * h:32 * (h + 1), 6, off:NT], v_st[:, j, k_head(h), :],
                                                PT[:, step % 3, h, off:NT], start=(j == 0), stop=(j == 4 * c + 3))
                    last.then_inc(s.pv_done, 1)

                def transpose_o(g, c):
                    wait(pe, s.o_copied, 2 * g + c + 1)
                    if c == 0:
                        wait(pe, s.normed, 2 * g)
                    elif isinstance(g, int) and g == L.groups - 1:
                        wait(pe, s.normed, 2 * g + 1)
                    else:
                        wait(pe, s.mT_copied, g + 2)
                    for i in range(4):
                        last = nc.tensor.transpose(PS[:, 7, i * P:(i + 1) * P], o_sb[:, i * P:(i + 1) * P], ident[:, :])
                    last.then_inc(s.ot_ready, 1)

                def transpose_max(g):
                    wait(pe, s.neg_ready, g + 1)
                    wait(pe, s.normed, 2 * g - 1)
                    nc.tensor.transpose(PSB[0:PARTS * HG * QB, 7, 0:P], neg_m[:, :, :, :].rearrange("p r h i -> p (r h i)"),
                                        ident_b[:, :]).then_inc(s.mT_ready, 1)

                def group(g, first=False, one_ahead=True, two_ahead=True):
                    for step in range(STEPS):
                        ahead = g + 1 if step < STEPS - LEAD else g + 2
                        units = UNIT_RUNS[(step + LEAD) % STEPS]
                        if not (one_ahead if step < STEPS - LEAD else two_ahead):
                            units = []
                        scores_T(g, step, 0)
                        scores(ahead, units[0:1])
                        scores_T(g, step, 1)
                        scores(ahead, units[1:2])
                        if step >= BEHIND:
                            weigh(g, step - BEHIND)
                        elif not first:
                            weigh(g - 1, step - BEHIND + STEPS)
                        scores(ahead, units[2:])
                        if step == 2 and not first:
                            transpose_o(g - 1, 1)
                        if step == 6:
                            transpose_o(g, 0)
                        if step == MT_STEP and one_ahead:
                            transpose_max(g + 1)

                past(pe, q.rotated if L.bias else q.qk_read, TILES)
                past(pe, q.v_read, TILES)
                past(pe, q.pt_copied, TILES * L.batches)
                scores(0, range(len(UNITS)))
                transpose_max(0)
                for run in range(LEAD):
                    scores(1, UNIT_RUNS[run])
                group(0, first=True)
                with pe.Fori(1, L.groups - 2) as g:
                    group(g)
                group(L.groups - 2, two_ahead=False)
                group(L.groups - 1, one_ahead=False, two_ahead=False)
                for step in range(STEPS - BEHIND, STEPS):
                    weigh(L.groups - 1, step)
                transpose_o(L.groups - 1, 1)

            def out_projection(s, w):
                open_counts(pe, s.t_ready, s.y_ready)
                with pe.Fori(0, CHUNKS) as c:
                    t0 = c * CHUNK
                    for u in range(CHUNK):
                        pe.wait_ge(s.at_ready, t0 + u + 1)
                        nc.tensor.transpose(PS[:, u, 0:P], xn[:, u, 0:P], ident[:, :])
                        nc.tensor.transpose(PS[:, u, P:DIM], xn[:, u, P:DIM], ident[:, :]).then_inc(s.t_ready, 1)
                    past(pe, s.x_added, t0)
                    for u in range(CHUNK):
                        pe.wait_ge(s.atT_ready, t0 + u + 1)
                        for k in range(KC):
                            last = nc.tensor.matmul(PS[:, 4 + u, 0:DIM], xnT[:, k, u * P:(u + 1) * P], w[:, k, :],
                                                    start=(k == 0), stop=(k == KC - 1))
                        last.then_inc(s.y_ready, 1)

            def feed_forward(f, wo):
                open_counts(pe, f.y_ready)

                def split_products(w, xs, out, start, stop):
                    for a, b in ((0, 0), (0, 1), (1, 0)):
                        mm = nc.tensor.matmul(out, w[a], xs[b], start=start and a + b == 0, stop=stop and a == 1)
                    return mm

                def transpose_x(c):
                    past(pe, f.x_low, KC * c)
                    for k in range(KC):
                        for u in range(CHUNK):
                            if k == 0:
                                pe.wait_ge(f.xn_ready, CHUNK * c + u + 1)
                            last = nc.tensor.transpose(PS[:, k, u * P:(u + 1) * P], xn[:, u, k * P:(k + 1) * P],
                                                       ident[:, :])
                        last.then_inc(f.xt_ready, 1)

                def gate_up(c):
                    for m in range(MC):
                        past(pe, f.h_ready, MC * c + max(0, m - 1))
                        for half in range(2):
                            col = half * INTER + m * P
                            for k in range(KC):
                                if m == 0 and half == 0:
                                    past(pe, f.x_low, KC * c + k + 1)
                                last = split_products([w[:, k, col:col + P] for w in w_gu_split],
                                                      [v[:, k, :] for v in xnT_split],
                                                      PS[:, 2 + 2 * (m % 2) + half, :], k == 0, k == KC - 1)
                        last.then_inc(f.gu_ready, 1)

                def down(c):
                    for u in range(CHUNK):
                        past(pe, f.x_added, CHUNK * c + max(0, u - 1))
                        for m in range(MC):
                            if u == 0:
                                past(pe, f.h_low, MC * c + m + 1)
                            last = split_products([h[:, m, u * P:(u + 1) * P] for h in h_split],
                                                  [w[:, m, :] for w in w_dn_split],
                                                  PS[:, 6 + u % 2, 0:DIM], m == 0, m == MC - 1)
                        last.then_inc(f.y_ready, 1)

                transpose_x(0)
                pe.wait_ge(wo.split_low, CHUNKS * SPLITS)
                with pe.Fori(0, CHUNKS - 1) as c:
                    gate_up(c)
                    transpose_x(c + 1)
                    down(c)
                gate_up(CHUNKS - 1)
                down(CHUNKS - 1)

            qkv(A, QKV["a"], w_qkv_a)
            transpose_weights()
            attention(A, ATT["a"], QKV["a"])
            out_projection(WO["a"], w_out_a)
            feed_forward(FFN[0], WO["a"])
            qkv(B, QKV["b"], w_qkv_b)
            attention(B, ATT["b"], QKV["b"])
            out_projection(WO["b"], w_out_b)
            feed_forward(FFN[1], WO["b"])


_INS = ["L0_attn_a_x", "L0_attn_a_wq", "L0_attn_a_wk", "L0_attn_a_wv", "L0_attn_a_wo",
        "L0_attn_b_Wq", "L0_attn_b_bq", "L0_attn_b_Wk", "L0_attn_b_bk", "L0_attn_b_Wv", "L0_attn_b_bv",
        "L0_attn_b_Wo", "L0_attn_b_bo", "L0_ffn_w_gate_up", "L0_ffn_w_down"]


def _rope_table(seq, d, theta=10000.0):
    import numpy as np

    freq = (np.float32(theta) ** (-(np.arange(d // 2, dtype=np.float32) * np.float32(2.0 / d)))).astype(np.float32)
    phase = np.arange(seq, dtype=np.float32)[:, None] * freq[None, :]
    cos, sin = np.cos(phase), np.sin(phase)
    table = np.concatenate([np.repeat(cos, 2, axis=1), np.stack([-sin, sin], axis=-1).reshape(seq, d)], axis=1)
    return np.ascontiguousarray(table.astype(np.float32))


def kernel(**inputs):
    import numpy as np
    import concourse.bacc as bacc
    from concourse.bass_utils import run_bass_kernel_spmd

    nc = bacc.Bacc("TRN2", target_bir_lowering=False, num_devices=1)
    arrays = {f"in_{n}": np.ascontiguousarray(inputs[n]) for n in _INS}
    arrays["rope_table"] = _rope_table(SEQ, DIM // 32)
    args = [nc.dram_tensor(n, a.shape, mybir.dt.from_np(a.dtype), kind="ExternalInput").ap()
            for n, a in arrays.items()]
    out = nc.dram_tensor("out", (BATCH, SEQ, DIM), F32, kind="ExternalOutput").ap()
    hybrid_layer(nc, *args, out)
    return run_bass_kernel_spmd(nc, [arrays], core_ids=[0]).results[0]["out"]
```

```python
from collections import namedtuple
from contextlib import ExitStack

import concourse.bass as bass
from concourse import mybir

F32 = mybir.dt.float32
F32R = mybir.dt.float32r
BF16 = mybir.dt.bfloat16
ALU = mybir.AluOpType
ACT = mybir.ActivationFunctionType
AX_X = mybir.AxisListType.X
ds = bass.ds

P = 128
BATCH, SEQ, DIM = 2, 1024, 256
TILES = BATCH * SEQ // P
KC = DIM // P
CHUNK = 4
CHUNKS = TILES // CHUNK
NT = CHUNK * P
INTER = 1024
MC = INTER // P
SPLITS = 3 * KC * INTER // NT // CHUNKS
EPS = 1e-5
NEG = -3.0e38
PARTS = 3
QB = SEQ // P
HG = 4
STEPS = 12
LEAD = 5
BEHIND = 2
MT_STEP = STEPS - LEAD + 1
MROW = 96
FIRST = (0, CHUNK)
EARLY = (0, TILES - CHUNK)
LATE_OF = {FIRST: (CHUNK, TILES), EARLY: (TILES - CHUNK, TILES)}
CHUNK_STEP = [(0, j) for j in range(4)] + [(1, j) for j in range(8)]
DIAGONAL = [s for s, (c, j) in enumerate(CHUNK_STEP) if j >= 4 * c]


class Attention:
    pass


def attention_shapes(heads, kv_heads, bias):
    a = Attention()
    d = a.d = DIM // heads
    a.heads, a.kv, a.bias = heads, kv_heads, bias
    a.kh = kv_heads * HG // heads
    a.groups = BATCH * heads // HG
    a.per_seq = heads // HG
    a.nq = heads * d
    a.nqk = (heads + kv_heads) * d
    a.nv = kv_heads * d
    a.row = PARTS * d
    a.blocks = -(-(heads + kv_heads) * a.row // P)
    a.batches = 1 if a.blocks <= 8 else 2
    
    if d == 8:
        a.q_runs = [(0, 3, 0), (0, 3, 24), (0, 3, 48)]
        a.k_runs = [(0, 3, 0), (1, 3, 24), (2, 3, 48)]
        a.scale = float(d) ** -0.5
    else:
        a.q_runs = [(0, 3, 0), (0, 2, 48), (0, 1, 80)]
        a.k_runs = [(0, 3, 0), (1, 2, 48), (2, 1, 80)]
        a.scale = float(d) ** -0.5
    a.loads = len(a.q_runs) + sum(n for _, n, _ in a.k_runs)
    return a


def max_units():
    units = []
    for i in range(QB):
        full = i // 4
        if full:
            units += [(i, 0, [h], 0, NT) for h in range(HG)]
        w = (i % 4 + 1) * P
        n = max(1, min(HG, NT // w))
        n = {4: 4, 2: 2, 1: 1}[n]
        units += [(i, full, list(range(h, h + n)), full * NT, w) for h in range(0, HG, n)]
    return units


UNITS = max_units()


UNITS_OF_STEP = [4, 3, 3, 2, 4, 4, 4, 4, 3, 3, 2, 2]


def unit_runs():
    counts = [UNITS_OF_STEP[(r - LEAD) % STEPS] for r in range(STEPS)]
    assert sum(counts) == len(UNITS)
    ends = [sum(counts[:r + 1]) for r in range(STEPS)]
    return [list(range(end - n, end)) for n, end in zip(counts, ends)]


UNIT_RUNS = unit_runs()
BEFORE = 7
FIRST_RUNS = [(1, list(range(BEFORE + s * (len(UNITS) - BEFORE) // (STEPS - LEAD),
                             BEFORE + (s + 1) * (len(UNITS) - BEFORE) // (STEPS - LEAD))))
              for s in range(STEPS - LEAD)] + [(2, run) for run in UNIT_RUNS[:LEAD]]


def wait(eng, sem, value):
    if not isinstance(value, int) or value > 0:
        eng.wait_ge(sem, value)


def past(eng, sem, count):
    if not isinstance(count, int) or count > 0:
        eng.wait_ge(sem, count + 1)


def open_counts(eng, *counts):
    for sem in counts:
        eng.nop().then_inc(sem, 1)


def hybrid_layer(nc, x_in, wq_a, wk_a, wv_a, wo_a, wq_b, bq_b, wk_b, bk_b, wv_b, bv_b, wo_b, bo_b,
                 w_gate_up, w_down, rope, out):
    A = attention_shapes(32, 8, False)
    B = attention_shapes(16, 16, True)
    x_rows = x_in.rearrange("b (t p) d -> p (b t) d", p=P)
    out_rows = out.rearrange("b (t p) d -> p (b t) d", p=P)
    scratch_a = nc.dram_tensor("scratch_a", (A.blocks * P, BATCH * SEQ), BF16).ap()
    scratch_m = nc.dram_tensor("scratch_m", (PARTS * HG * QB, P), BF16).ap()
    scratch_b = nc.dram_tensor("scratch_b", (B.blocks * P, BATCH * SEQ), BF16).ap()

    with ExitStack() as ctx:
        def sb(name, shape, dt=F32):
            return ctx.enter_context(nc.sbuf_tensor(name, shape, dt))

        def sems(prefix, names):
            return namedtuple(prefix, names)(*[ctx.enter_context(nc.semaphore(f"{prefix}_{n}"))
                                               for n in names.split()])

        PS = ctx.enter_context(nc.psum_tensor("PS", [P, 8, NT], F32))
        PSB = PS[:, :, :].bitcast(BF16)

        x = sb("x", [P, TILES, DIM])
        stats = sb("stats", [P, TILES, 6])
        mean_var = sb("mean_var", [P, TILES, 2])
        spread = sb("spread", [P, TILES])
        rstd = sb("rstd", [P, TILES])
        eps = sb("eps", [P, 1])
        w_qkv_a = sb("w_qkv_a", [P, KC, A.nqk + A.nv])
        w_out_a = sb("w_out_a", [P, KC, DIM])
        w_qkv_b = sb("w_qkv_b", [P, KC, 3 * DIM])
        w_out_b = sb("w_out_b", [P, KC, DIM])
        w_ffn = sb("w_ffn", [P, (2 * KC + KC) * INTER])
        w_gu = w_ffn[:, 0:2 * KC * INTER].rearrange("p (k n) -> p k n", k=KC)
        w_dn = w_ffn[:, 2 * KC * INTER:].rearrange("p (m n) -> p m n", m=MC)
        bias_qkv = sb("bias_qkv", [P, 3 * DIM])
        bias_out = sb("bias_out", [P, DIM])
        rope_sb = sb("rope_sb", [P, QB, 2 * A.d])
        ident = sb("ident", [P, P])
        ident_b = sb("ident_b", [P, P], BF16)
        mask_b = sb("mask_b", [P, P], BF16)
        v_st = sb("v_st", [P, QB, HG, 32])
        mx = sb("mx", [P, 2, QB, HG])
        neg_rest = sb("neg_rest", [P, QB, HG])
        neg_m = sb("neg_m", [P, PARTS, HG, QB], BF16)
        mT = sb("mT", [PARTS * HG * QB, P], BF16)
        o_sb = sb("o_sb", [P, NT])
        rden = sb("rden", [P, 4, HG, 1])
        raw_b = sb("raw_b", [P, 4, KC, DIM])
        xn = sb("xn", [P, CHUNK, DIM])
        xnT = sb("xnT", [P, KC, NT])
        qk = sb("qk", [P, 2, 2 * DIM])
        qk_rest = sb("qk_rest", [P, 2, 2 * DIM])
        qk_rot = sb("qk_rot", [P, A.nqk])
        parts = sb("parts", [P, 2, B.blocks * P], BF16)

        with ExitStack() as attention_ctx:
            def att_sb(name, shape, dt=F32):
                return attention_ctx.enter_context(nc.sbuf_tensor(name, shape, dt))

            QT = att_sb("QT", [P, 3, HG * SEQ], BF16)
            KT = att_sb("KT", [P, 3, HG * SEQ], BF16)
            v_all = att_sb("v_all", [P, TILES, DIM])
            attn_mem = att_sb("attn_mem", [P, TILES * DIM])
            work = att_sb("work", [P, 3 * HG * NT])
        attn = attn_mem[:, :].rearrange("p (t n) -> p t n", t=TILES)
        parts_T = attn_mem[:, 0:B.blocks * NT // 2].bitcast(BF16).rearrange("p (b t) -> p b t", b=B.blocks)
        PT = work[:, :].rearrange("p (s h q) -> p s h q", s=3, h=HG)
        raw_gu = work[:, 0:16 * DIM].rearrange("p (o n) -> p o n", o=16)
        raw_dn = work[:, 16 * DIM:16 * DIM + 2 * INTER].rearrange("p (o n) -> p o n", o=2)
        w_split = [sb("w_high", [P, 3 * KC * INTER], F32R), sb("w_low", [P, 3 * KC * INTER], F32R)]
        xnT_split = [sb("xnT_high", [P, KC, NT], F32R), sb("xnT_low", [P, KC, NT], F32R)]
        h_split = [sb("h_high", [P, MC, NT], F32R), sb("h_low", [P, MC, NT], F32R)]
        gate_sb = sb("gate_sb", [P, 2, NT])
        h_sb = sb("h_sb", [P, 2, NT])
        w_gu_split = [w[:, 0:2 * KC * INTER].rearrange("p (k n) -> p k n", k=KC) for w in w_split]
        w_dn_split = [w[:, 2 * KC * INTER:3 * KC * INTER].rearrange("p (m n) -> p m n", m=MC) for w in w_split]

        WEIGHT_BANKS_OF = [[raw_gu[:, o + i, k * P:(k + 1) * P] for i in range(4)]
                           for k in range(KC) for o in range(0, 2 * INTER // P, 4)]
        WEIGHT_BANKS_TO = [w_gu[:, k, o * P:(o + 4) * P] for k in range(KC) for o in range(0, 2 * INTER // P, 4)]
        WEIGHT_BANKS_OF += [[raw_dn[:, o, (m + i) * P:(m + i + 1) * P] for i in range(2) for o in range(KC)]
                            for m in range(0, MC, 2)]
        WEIGHT_BANKS_TO += [w_dn[:, m:m + 2, :].rearrange("p m n -> p (m n)") for m in range(0, MC, 2)]
        WEIGHT_BANKS_OF += [[raw_b[:, n, o, k * P:(k + 1) * P] for k in range(KC) for o in range(KC)]
                            for n in range(4)]
        WEIGHT_BANKS_TO += [w_qkv_b[:, :, n * DIM:(n + 1) * DIM] for n in range(3)] + [w_out_b[:, :, :]]

        def by_head(L, buffer, u):
            return buffer[:, u % 2, 0:L.nqk].rearrange("p (h d) -> p h d", d=L.d)

        def part(L, u):
            return parts[:, u % 2, 0:(L.heads + L.kv) * L.row].rearrange("p (h r d) -> p h r d", r=PARTS, d=L.d)

        s_in = sems("start", "wa wo_a rope wb wgu bias zero const pad ones padded_again raw_T raw_copied")
        s_x = sems("x", " ".join(f"chunk{c}" for c in range(CHUNKS)))
        LN = [sems(f"ln{n}", "stats aggregated spread ready") for n in range(4)]
        qkv_names = ("xn_ready xt_ready xnT_ready qkv_ready qk_read v_read own rotated part0 rest part1 parts_ready "
                     "pt_ready pt_copied stored_even stored_odd")
        att_names = ("loaded m_stored m_loaded s_ready s_reduced st_ready exp_done masked pv_done v_staged o_copied "
                     "ot_ready rden_ready normed neg_step neg_ready mT_ready mT_copied")
        QKV = {L: sems(f"qkv_{L}", qkv_names) for L in "ab"}
        ATT = {L: sems(f"att_{L}", att_names) for L in "ab"}
        WO = {L: sems(f"wo_{L}", "split_high split_low at_ready t_ready atT_ready y_ready bias_added x_added") for L in "ab"}
        FFN = [sems(f"ffn{n}", "xn_ready xt_ready x_high x_low gu_ready silu_done h_ready h_high h_low y_ready x_added")
               for n in range(2)]
        s_out = sems("out", "stored")

        block = ctx.enter_context(nc.Block())

        @block.sync
        def _(sp):
            for q in (QKV["a"], QKV["b"]):
                open_counts(sp, q.stored_even, q.stored_odd)
            for c in range(CHUNKS):
                sp.dma_start(x[:, c * CHUNK:(c + 1) * CHUNK, :],
                             x_rows[:, c * CHUNK:(c + 1) * CHUNK, :]).then_inc(s_x[c], 16)
            sp.dma_start(w_out_a[:, :, :], wo_a.rearrange("(k p) n -> p k n", p=P)).then_inc(s_in.wo_a, 16)
            for c in range(CHUNKS):
                sp.wait_ge(s_x[c], 16)
            sp.dma_start(raw_gu, w_gate_up.rearrange("(o p) n -> p o n", p=P)).then_inc(s_in.wgu, 16)
            sp.dma_start(raw_dn, w_down.rearrange("(o p) n -> p o n", p=P)).then_inc(s_in.wgu, 16)
            for n, w in enumerate((wq_b, wk_b, wv_b, wo_b)):
                sp.dma_start(raw_b[:, n, :, :], w.rearrange("(o p) n -> p o n", p=P)).then_inc(s_in.wb, 16)
            for n, b in enumerate((bq_b, bk_b, bv_b)):
                sp.dma_start(bias_qkv[:, n * DIM:(n + 1) * DIM], b.partition_broadcast(P)).then_inc(s_in.bias, 16)
            sp.dma_start(bias_out[:, :], bo_b.partition_broadcast(P)).then_inc(s_in.bias, 16)

            def store_parts(L, q, scratch, chunks):
                rows = scratch.rearrange("(b p) t -> p b t", p=P)
                with sp.Fori(*chunks) as c:
                    for half, stored in enumerate((q.stored_even, q.stored_odd)):
                        past(sp, q.pt_copied, (c * CHUNK + (half + 1) * CHUNK // 2) * L.batches)
                        sp.dma_start(rows[:, :, ds(c * NT + half * NT // 2, NT // 2)],
                                     parts_T[:, 0:L.blocks, half * NT // 2:(half + 1) * NT // 2]).then_inc(stored, 16)

            def attention(L, s, q, scratch):
                def load(g):
                    seq, j = g // L.per_seq, g % L.per_seq
                    wait(sp, s.st_ready, 2 * STEPS * (g - 2))
                    wait(sp, s.loaded, 16 * L.loads * g)
                    q_src = scratch[ds(j * (HG * L.row), HG * L.row), ds(seq * SEQ, SEQ)]
                    q_src = q_src.rearrange("(h r) t -> r h t", h=HG)
                    k_src = scratch[ds(j * (L.kh * L.row) + L.heads * L.row, L.kh * L.row), ds(seq * SEQ, SEQ)]
                    k_src = k_src.rearrange("(h r) t -> r h t", h=L.kh)
                    for part, n, row in L.q_runs:
                        dst = QT[row:row + n * L.d, ds(g % 3, 1), :].rearrange("p x (h t) -> p (x h) t", h=HG)
                        sp.dma_start(dst, q_src[part * L.d:(part + n) * L.d, :, :]).then_inc(s.loaded, 16)
                    for part, n, row in L.k_runs:
                        for r in range(n):
                            dst = KT[row + r * L.d:row + (r + 1) * L.d, ds(g % 3, 1), 0:L.kh * SEQ]
                            sp.dma_start(dst.rearrange("p x (h t) -> p (x h) t", h=L.kh),
                                         k_src[part * L.d:(part + 1) * L.d, :, :]).then_inc(s.loaded, 16)

                def load_max(g):
                    sp.wait_ge(s.mT_copied, g + 1)
                    sp.dma_start(scratch_m, mT[:, :]).then_inc(s.m_stored, 16)
                    sp.wait_ge(s.m_stored, g * 16 + 16)
                    sp.dma_start(QT[MROW:MROW + PARTS, ds(g % 3, 1), :].rearrange("p x n -> p (x n)"),
                                 scratch_m.rearrange("(r x) t -> r (x t)", r=PARTS)).then_inc(s.m_loaded, 16)

                def group(g, second=True):
                    if second:
                        load(g + 2)
                    load_max(g + 1)

                store_parts(L, q, scratch, (0, CHUNKS // BATCH))
                past(sp, q.stored_even, 16 * CHUNKS // BATCH)
                past(sp, q.stored_odd, 16 * CHUNKS // BATCH)
                sp.wait_ge(s_in.ones, 2)
                if L is B:
                    sp.wait_ge(s_in.padded_again, 3)
                load(0)
                store_parts(L, q, scratch, (CHUNKS // BATCH, CHUNKS))
                load(1)
                past(sp, q.stored_even, 16 * CHUNKS)
                past(sp, q.stored_odd, 16 * CHUNKS)
                load_max(0)
                group(0)
                with sp.Fori(1, L.groups - 2) as g:
                    group(g)
                group(L.groups - 2, second=False)

            attention(A, ATT["a"], QKV["a"], scratch_a)
            attention(B, ATT["b"], QKV["b"], scratch_b)
            with sp.Fori(0, CHUNKS) as c:
                past(sp, FFN[1].x_added, c * CHUNK + CHUNK)
                sp.dma_start(out_rows[:, ds(c * CHUNK, CHUNK), :], x[:, ds(c * CHUNK, CHUNK), :])\
                    .then_inc(s_out.stored, 16)
            sp.wait_ge(s_out.stored, 16 * CHUNKS)

        @block.gpsimd
        def _(pool):
            nc.gpsimd.memset(ident[:, :], 1.0).then_inc(s_in.zero, 1)
            nc.gpsimd.memset(mask_b[:, :], 0.0).then_inc(s_in.zero, 1)
            pool.wait_ge(s_in.zero, 2)
            nc.gpsimd.affine_select(out=ident[:, :], in_=ident[:, :], compare_op=ALU.is_equal, fill=0.0, base=0,
                                    pattern=[[-1, P]], channel_multiplier=1).then_inc(s_in.zero, 1)
            nc.gpsimd.affine_select(out=mask_b[:, :], in_=mask_b[:, :], compare_op=ALU.is_ge, fill=NEG, base=0,
                                    pattern=[[-1, P]], channel_multiplier=1).then_inc(s_in.const, 1)
            pool.wait_ge(s_in.zero, 3)
            nc.gpsimd.tensor_copy(ident_b[:, :], ident[:, :]).then_inc(s_in.const, 1)
            nc.gpsimd.memset(QT[:, :, :].bitcast(F32), 0.0).then_inc(s_in.pad, 1)
            nc.gpsimd.memset(KT[:, :, :].bitcast(F32), 0.0).then_inc(s_in.pad, 1)
            nc.gpsimd.memset(v_st[:, :, :, :], 0.0).then_inc(s_in.pad, 1)
            pool.wait_ge(s_in.pad, 3)
            nc.gpsimd.memset(KT[MROW:MROW + PARTS, :, :], 1.0).then_inc(s_in.ones, 1)
            pool.wait_ge(s_in.ones, 1)
            nc.gpsimd.memset(v_st[:, :, :, A.d:A.d + 1], 1.0).then_inc(s_in.ones, 1)

            def attention(L, s):
                with pool.Fori(0, L.groups) as g:
                    for step in DIAGONAL:
                        c, j = CHUNK_STEP[step]
                        off = (j - 4 * c) * P
                        pool.wait_ge(s.exp_done, g * (2 * STEPS) + 2 * step + 2)
                        pool.nop(nofuse=True)
                        t = PT[:, step % 3, :, off:off + P]
                        nc.gpsimd.affine_select(out=t, in_=t, compare_op=ALU.is_ge, fill=0.0, base=0,
                                                pattern=[[0, HG], [1, P]], channel_multiplier=-1)\
                            .then_inc(s.masked, 1)

            def split_low(s):
                for n in range(CHUNKS * SPLITS):
                    pool.wait_ge(s.split_high, n + 1)
                    piece = slice(n * NT, (n + 1) * NT)
                    nc.gpsimd.tensor_tensor(w_split[1][:, piece], w_ffn[:, piece], w_split[0][:, piece].bitcast(F32),
                                            ALU.subtract).then_inc(s.split_low, 1)

            attention(A, ATT["a"])
            split_low(WO["a"])
            past(pool, FFN[0].x_added, TILES)
            nc.gpsimd.memset(QT[:, :, :].bitcast(F32), 0.0).then_inc(s_in.padded_again, 1)
            nc.gpsimd.memset(KT[:, :, :].bitcast(F32), 0.0).then_inc(s_in.padded_again, 1)
            pool.wait_ge(s_in.padded_again, 2)
            nc.gpsimd.memset(KT[MROW:MROW + PARTS, :, :], 1.0).then_inc(s_in.padded_again, 1)
            attention(B, ATT["b"])
            split_low(WO["b"])

        @block.scalar
        def _(act):
            for q in (QKV["a"], QKV["b"]):
                open_counts(act, q.xnT_ready, q.pt_copied)
            for f in FFN:
                open_counts(act, f.x_high)
            for dst, src in ((w_qkv_a[:, :, 0:A.nq], wq_a), (w_qkv_a[:, :, A.nq:A.nqk], wk_a),
                             (w_qkv_a[:, :, A.nqk:A.nqk + A.nv], wv_a)):
                act.dma_start(dst, src.rearrange("(k p) n -> p k n", p=P)).then_inc(s_in.wa, 16)
            act.dma_start(rope_sb[:, :, :], rope.rearrange("(t p) n -> p t n", p=P)).then_inc(s_in.rope, 16)

            def spread_of(ln, tiles):
                act.wait_ge(ln.aggregated, tiles[1])
                nc.scalar.activation(spread[:, tiles[0]:tiles[1]], mean_var[:, tiles[0]:tiles[1], 1], ACT.Sqrt,
                                     bias=eps[:, 0:1]).then_inc(ln.spread, 1)

            def qkv(L, q):
                def copy_xT(t0, u):
                    past(act, q.xt_ready, t0 + u + 1)
                    slot = u % CHUNK
                    nc.scalar.activation(xnT[:, :, slot * P:(slot + 1) * P],
                                         PS[:, u % 2, 0:DIM].rearrange("p (k t) -> p k t", k=KC),
                                         ACT.Copy).then_inc(q.xnT_ready, 1)

                def part0(t0, u):
                    past(act, q.rotated, t0 + u + 1)
                    past(act, q.pt_ready, (t0 + max(0, u - 1)) * L.batches)
                    nc.scalar.activation(part(L, u)[:, :, 0, :], by_head(L, qk, u), ACT.Copy).then_inc(q.part0, 1)

                def part1(t0, u):
                    act.wait_ge(q.rest, t0 + u + 1)
                    nc.scalar.activation(part(L, u)[:, :, 1, :], by_head(L, qk_rest, u), ACT.Copy).then_inc(q.part1, 1)

                def copy_parts(t0, u):
                    n = L.blocks // L.batches
                    for k in range(L.batches):
                        past(act, q.pt_ready, (t0 + u) * L.batches + k + 1)
                        if u % 2 == 0 and k == 0:
                            past(act, (q.stored_even, q.stored_odd)[u // 2], t0 // CHUNK * 16)
                        bank = 6 + (u * L.batches + k) % 2
                        nc.scalar.activation(parts_T[:, k * n:(k + 1) * n, u * P:(u + 1) * P],
                                             PSB[:, bank, 0:n * P].rearrange("p (b t) -> p b t", b=n),
                                             ACT.Copy).then_inc(q.pt_copied, 1)

                def chunk(t0, last=False):
                    for u in range(CHUNK):
                        if not last or u + 1 < CHUNK:
                            part0(t0, u + 1)
                            part1(t0, u + 1)
                        if not last:
                            copy_xT(t0, u + 4)
                        copy_parts(t0, u)

                for u in range(4):
                    copy_xT(0, u)
                if L is A:
                    spread_of(LN[0], LATE_OF[FIRST])
                else:
                    spread_of(LN[2], LATE_OF[EARLY])
                part0(0, 0)
                part1(0, 0)
                with act.Fori(0, CHUNKS - 1) as c:
                    chunk(c * CHUNK)
                chunk((CHUNKS - 1) * CHUNK, last=True)

            def transposed_weights():
                for n, dst in enumerate(WEIGHT_BANKS_TO):
                    act.wait_ge(s_in.raw_T, n + 1)
                    src = PS[:, n % 4, :]
                    if len(dst.shape) == 3:
                        src = src.rearrange("p (k c) -> p k c", k=KC)
                    nc.scalar.activation(dst, src, ACT.Copy).then_inc(s_in.raw_copied, 1)

            def attention(L, s):
                def copy_o(g, c):
                    wait(act, s.pv_done, STEPS * g + (4, STEPS)[c])
                    wait(act, s.ot_ready, 2 * g + c)
                    nc.scalar.activation(o_sb[:, :], PS[:, 6, :], ACT.Copy).then_inc(s.o_copied, 1)

                def copy_mT(g):
                    wait(act, s.mT_ready, g + 1)
                    wait(act, s.m_loaded, 16 * g)
                    nc.scalar.activation(mT[:, :], PSB[0:PARTS * HG * QB, 7, 0:P], ACT.Copy).then_inc(s.mT_copied, 1)

                def group(g, first=False, last=False):
                    for step, (c, j) in enumerate(CHUNK_STEP):
                        off = max(0, j - 4 * c) * P
                        wait(act, s.pv_done, STEPS * g + step - 2)
                        for half in range(2):
                            wait(act, s.st_ready, 2 * STEPS * g + 2 * step + half + 1)
                            nc.scalar.activation(PT[:, step % 3, 2 * half:2 * half + 2, off:NT],
                                                 PS[:, 2 * half:2 * half + 2, off:NT], ACT.Exp,
                                                 scale=L.scale).then_inc(s.exp_done, 1)
                        if step == BEHIND - 1 and not first:
                            copy_o(g - 1, 1)
                        if step == BEHIND + 3:
                            copy_o(g, 0)
                        if step == MT_STEP and not last:
                            copy_mT(g + 1)

                copy_mT(0)
                group(0, first=True)
                with act.Fori(1, L.groups - 1) as g:
                    group(g)
                group(L.groups - 1, last=True)
                copy_o(L.groups - 1, 1)

            def out_projection(s, att, L):
                def chunk(c):
                    past(act, s.t_ready, c * CHUNK)
                    for u in range(CHUNK):
                        nc.scalar.activation(xn[:, u, :], attn[:, ds(c * CHUNK + u, 1), :].rearrange("p x n -> p (x n)"),
                                             ACT.Copy).then_inc(s.at_ready, 1)
                    for i in range(SPLITS):
                        piece = ds(c * (SPLITS * NT) + i * NT, NT)
                        nc.scalar.activation(w_split[0][:, piece], w_ffn[:, piece], ACT.Copy).then_inc(s.split_high, 1)

                act.wait_ge(att.normed, 2 * L.groups - 1)
                with act.Fori(0, CHUNKS - 1) as c:
                    chunk(c)
                act.wait_ge(att.normed, 2 * L.groups)
                chunk(CHUNKS - 1)

            def feed_forward(f, ln_own, ln):
                def x_high(c):
                    for k in range(KC):
                        act.wait_ge(f.xt_ready, KC * c + k + 1)
                        nc.scalar.activation(xnT_split[0][:, k, :], PS[:, k, :], ACT.Copy).then_inc(f.x_high, 1)

                def h_high(c, m):
                    past(act, f.h_ready, MC * c + m + 1)
                    nc.scalar.activation(h_split[0][:, m, :], h_sb[:, m % 2, :], ACT.Copy).then_inc(f.h_high, 1)

                def chunk(c, last=False):
                    for m in range(MC):
                        act.wait_ge(f.gu_ready, MC * c + m + 1)
                        past(act, f.h_ready, MC * c + max(0, m - 1))
                        nc.scalar.activation(gate_sb[:, m % 2, :], PS[:, 2 + 2 * (m % 2), :],
                                             ACT.Silu).then_inc(f.silu_done, 1)
                        if m > 0:
                            h_high(c, m - 1)
                        if last and ln is not None and m == 2:
                            spread_of(ln, EARLY)
                    h_high(c, MC - 1)
                    if not last:
                        x_high(c + 1)

                x_high(0)
                spread_of(ln_own, LATE_OF[EARLY])
                with act.Fori(0, CHUNKS - 1) as c:
                    chunk(c)
                chunk(CHUNKS - 1, last=True)

            spread_of(LN[0], FIRST)
            qkv(A, QKV["a"])
            transposed_weights()
            attention(A, ATT["a"])
            out_projection(WO["a"], ATT["a"], A)
            spread_of(LN[1], EARLY)
            feed_forward(FFN[0], LN[1], LN[2])
            qkv(B, QKV["b"])
            attention(B, ATT["b"])
            out_projection(WO["b"], ATT["b"], B)
            spread_of(LN[3], EARLY)
            feed_forward(FFN[1], LN[3], None)

        @block.vector
        def _(dve):
            for q in (QKV["a"], QKV["b"]):
                open_counts(dve, q.qk_read, q.v_read, q.rotated, q.parts_ready)
            for s in (WO["a"], WO["b"]):
                open_counts(dve, s.x_added)
            for f in FFN:
                open_counts(dve, f.x_low, f.h_ready, f.h_low, f.x_added)
            nc.vector.memset(eps[:, :], EPS).then_inc(s_in.const, 1)
            nc.vector.memset(parts[:, :, :], 0.0).then_inc(s_in.const, 1)

            def aggregate(ln, tiles):
                dve.wait_ge(ln.stats, tiles[1])
                for t in range(*tiles):
                    nc.vector.bn_aggr(mean_var[:, t, :], stats[:, t, :]).then_inc(ln.aggregated, 1)

            def factors(ln, tiles):
                n = 1 if tiles[0] == 0 else 2
                dve.wait_ge(ln.spread, n)
                nc.vector.reciprocal(rstd[:, tiles[0]:tiles[1]], spread[:, tiles[0]:tiles[1]]).then_inc(ln.ready, 1)
                dve.wait_ge(ln.ready, n)

            def x_tile(t):
                return x[:, ds(t, 1), :].rearrange("p x n -> p (x n)")

            def normed(dst, t):
                return nc.vector.tensor_scalar(dst, x_tile(t), mean_var[:, ds(t, 1), 0], rstd[:, ds(t, 1)],
                                               ALU.subtract, ALU.mult)

            def norm_qkv(q, t0, u):
                if u >= CHUNK:
                    past(dve, q.xt_ready, t0 + u - CHUNK + 1)
                normed(xn[:, u % CHUNK, :], t0 + u).then_inc(q.xn_ready, 1)

            def qkv(L, q):
                H = L.heads + L.kv

                def project(t0, u):
                    t = t0 + u
                    src = PS[:, 2 + 2 * (u % 2), 0:L.nqk]
                    r = qk[:, u % 2, 0:L.nqk]
                    past(dve, q.qkv_ready, t + 1)
                    past(dve, q.parts_ready, t0 + max(0, u - 1))
                    if L.bias:
                        nc.vector.tensor_tensor(r, src, bias_qkv[:, 0:L.nqk], ALU.add).then_inc(q.rotated, 1)
                        nc.vector.tensor_tensor(v_all[:, ds(t, 1), :].rearrange("p x n -> p (x n)"),
                                                PS[:, 3 + 2 * (u % 2), 0:L.nv], bias_qkv[:, L.nqk:L.nqk + L.nv],
                                                ALU.add).then_inc(q.v_read, 1)
                        return
                    cos = rope_sb[:, ds(t % QB, 1), 0:L.d].broadcast_to([P, H, L.d])
                    nc.vector.tensor_tensor(r.rearrange("p (h d) -> p h d", d=L.d),
                                            src.rearrange("p (h d) -> p h d", d=L.d), cos,
                                            ALU.mult).then_inc(q.own, 1)
                    past(dve, q.rotated, t)
                    pairs = "p (h d e) -> p h d e"
                    rot = qk_rot[:, :].rearrange(pairs, h=H, e=2)
                    raw = src.rearrange(pairs, h=H, e=2)
                    sin = rope_sb[:, ds(t % QB, 1), L.d:2 * L.d].rearrange("p x (d e) -> p x d e", e=2)
                    nc.vector.tensor_tensor(rot[:, :, :, 0], raw[:, :, :, 1],
                                            sin[:, :, :, 0].broadcast_to([P, H, L.d // 2]),
                                            ALU.mult).then_inc(q.own, 1)
                    nc.vector.tensor_tensor(rot[:, :, :, 1], raw[:, :, :, 0],
                                            sin[:, :, :, 1].broadcast_to([P, H, L.d // 2]),
                                            ALU.mult).then_inc(q.qk_read, 1)
                    nc.vector.tensor_copy(v_all[:, ds(t, 1), 0:L.nv].rearrange("p x n -> p (x n)"),
                                          PS[:, 2 + 2 * (u % 2), L.nqk:L.nqk + L.nv]).then_inc(q.v_read, 1)
                    dve.wait_ge(q.own, t * 2 + 2)
                    past(dve, q.qk_read, t + 1)
                    nc.vector.tensor_tensor(r, r, qk_rot[:, :], ALU.add).then_inc(q.rotated, 1)

                def rest(t0, u):
                    dve.wait_ge(q.part0, t0 + u + 1)
                    nc.vector.tensor_tensor(by_head(L, qk_rest, u), by_head(L, qk, u), part(L, u)[:, :, 0, :],
                                            ALU.subtract).then_inc(q.rest, 1)

                def part2(t0, u):
                    dve.wait_ge(q.part1, t0 + u + 1)
                    nc.vector.tensor_tensor(part(L, u)[:, :, 2, :], by_head(L, qk_rest, u), part(L, u)[:, :, 1, :],
                                            ALU.subtract).then_inc(q.parts_ready, 1)

                def chunk(t0, last=False):
                    for u in range(CHUNK):
                        more = not last or u + 1 < CHUNK
                        if more:
                            project(t0, u + 1)
                        part2(t0, u)
                        if not last:
                            norm_qkv(q, t0, u + 4)
                        if more:
                            rest(t0, u + 1)

                project(0, 0)
                if L is B:
                    factors(LN[2], LATE_OF[EARLY])
                rest(0, 0)
                with dve.Fori(0, CHUNKS - 1) as c:
                    chunk(c * CHUNK)
                chunk((CHUNKS - 1) * CHUNK, last=True)

            def attention(L, s, q):
                D = L.d

                def reduce_units(g, units, negating=None):
                    for x0, n in enumerate(units):
                        if negating is not None and 0 < x0 < PARTS:
                            negate_parts(negating, x0)
                        i, which, heads, k0, w = UNITS[n]
                        if n == 0:
                            wait(dve, s.neg_step, 4 * g - 1)
                        wait(dve, s.s_ready, len(UNITS) * g + n + 1)
                        nc.vector.tensor_reduce(mx[:, which, i, heads[0]:heads[0] + len(heads)],
                                                PS[:, 4 + n % 2, 0:len(heads) * w].rearrange("p (h k) -> p h k", k=w),
                                                axis=AX_X, op=ALU.max).then_inc(s.s_reduced, 1)

                def negate_max(g):
                    wait(dve, s.s_reduced, len(UNITS) * (g + 1))
                    nc.vector.tensor_tensor(mx[:, 0, 4:8, :], mx[:, 0, 4:8, :], mx[:, 1, 4:8, :],
                                            ALU.max).then_inc(s.neg_step, 1)
                    m = mx[:, 0, :, :].rearrange("p i h -> p h i")
                    rest = neg_rest[:, :, :].rearrange("p i h -> p h i")
                    wait(dve, s.neg_step, 4 * g + 1)
                    wait(dve, s.mT_ready, g)
                    nc.vector.tensor_scalar(neg_m[:, 0, :, :], m, -1.0, None, ALU.mult).then_inc(s.neg_step, 1)
                    wait(dve, s.neg_step, 4 * g + 2)
                    nc.vector.scalar_tensor_tensor(out=rest, in0=m, scalar=-1.0, in1=neg_m[:, 0, :, :],
                                                   op0=ALU.mult, op1=ALU.subtract).then_inc(s.neg_step, 1)

                def negate_parts(g, part):
                    rest = neg_rest[:, :, :].rearrange("p i h -> p h i")
                    wait(dve, s.neg_step, 4 * g + 2 + part)
                    if part == 1:
                        nc.vector.tensor_copy(neg_m[:, 1, :, :], rest).then_inc(s.neg_step, 1)
                    else:
                        nc.vector.tensor_tensor(neg_m[:, 2, :, :], rest, neg_m[:, 1, :, :],
                                                ALU.subtract).then_inc(s.neg_ready, 1)

                def stage_v(g):
                    wait(dve, s.pv_done, STEPS * g)
                    src = v_all[:, ds((g // L.per_seq) * QB, QB), ds((g % L.per_seq) * (L.kh * D), L.kh * D)]
                    nc.vector.tensor_copy(v_st[:, :, 0:L.kh, 0:D],
                                          src.rearrange("p t (h d) -> p t h d", d=D)).then_inc(s.v_staged, 1)

                def normalise(g, c):
                    wait(dve, s.ot_ready, 2 * g + c + 1)
                    o = PS[:, 7, :].rearrange("p (t h r) -> p t h r", t=4, h=HG)
                    wait(dve, s.normed, 2 * g + c)
                    nc.vector.reciprocal(rden[:, :, :, :], o[:, :, :, D:D + 1]).then_inc(s.rden_ready, 1)
                    wait(dve, s.rden_ready, 2 * g + c + 1)
                    dst = attn[:, ds((g // L.per_seq) * QB + 4 * c, 4), ds((g % L.per_seq) * (HG * D), HG * D)]
                    nc.vector.tensor_tensor(dst.rearrange("p t (h d) -> p t h d", d=D), o[:, :, :, 0:D],
                                            rden[:, :, :, :].broadcast_to([P, 4, HG, D]),
                                            ALU.mult).then_inc(s.normed, 1)

                def group(g, first=False, one_ahead=True, two_ahead=True):
                    for step in range(STEPS):
                        negating = g + 1 if step == STEPS - LEAD else None
                        if first:
                            reduce_units(*FIRST_RUNS[step], negating)
                        elif step < STEPS - LEAD:
                            if one_ahead:
                                reduce_units(g + 1, UNIT_RUNS[step + LEAD])
                        elif two_ahead:
                            reduce_units(g + 2, UNIT_RUNS[step + LEAD - STEPS], negating)
                        elif one_ahead and negating is not None:
                            for part in range(1, PARTS):
                                negate_parts(negating, part)
                        if step == BEHIND - 1:
                            stage_v(g)
                        if step == 3 and not first:
                            normalise(g - 1, 1)
                        if step == STEPS - LEAD - 1 and one_ahead:
                            negate_max(g + 1)
                        if step == 7:
                            if first:
                                past(dve, q.stored_even, 16 * CHUNKS)
                                past(dve, q.stored_odd, 16 * CHUNKS)
                            normalise(g, 0)

                past(dve, q.v_read, TILES)
                if L is B:
                    nc.vector.memset(v_st[:, :, :, D:D + 1], 1.0).then_inc(s_in.ones, 1)
                reduce_units(0, range(len(UNITS)))
                negate_max(0)
                for part in range(1, PARTS):
                    negate_parts(0, part)
                reduce_units(1, range(BEFORE))
                group(0, first=True)
                with dve.Fori(1, L.groups - 2) as g:
                    group(g)
                group(L.groups - 2, two_ahead=False)
                group(L.groups - 1, one_ahead=False, two_ahead=False)
                normalise(L.groups - 1, 1)

            def norm_ffn(f, c, u):
                wait(dve, f.xt_ready, KC * c)
                normed(xn[:, u, :], c * CHUNK + u).then_inc(f.xn_ready, 1)

            def x_low(f, c):
                for k in range(KC):
                    past(dve, f.x_high, KC * c + k + 1)
                    nc.vector.tensor_tensor(xnT_split[1][:, k, :], PS[:, k, :], xnT_split[0][:, k, :].bitcast(F32),
                                            ALU.subtract).then_inc(f.x_low, 1)

            def out_projection(s, ln, bias, f):
                def copy_attn_T(c, u):
                    past(dve, s.t_ready, c * CHUNK + u + 1)
                    nc.vector.tensor_copy(xnT[:, :, u * P:(u + 1) * P],
                                          PS[:, u, 0:DIM].rearrange("p (k t) -> p k t", k=KC))\
                        .then_inc(s.atT_ready, 1)

                def chunk(c, last=False):
                    t0 = c * CHUNK
                    if bias:
                        for u in range(CHUNK):
                            nc.vector.tensor_tensor(x_tile(t0 + u), x_tile(t0 + u), bias_out[:, :],
                                                    ALU.add).then_inc(s.bias_added, 1)
                    if last:
                        past(dve, s.t_ready, TILES)
                        factors(ln, EARLY)
                        for u in range(CHUNK):
                            norm_ffn(f, 0, u)
                    for u in range(CHUNK):
                        past(dve, s.y_ready, t0 + u + 1)
                        if bias:
                            dve.wait_ge(s.bias_added, t0 + u + 1)
                        nc.vector.tensor_tensor(x_tile(t0 + u), x_tile(t0 + u), PS[:, 4 + u, 0:DIM],
                                                ALU.add).then_inc(s.x_added, 1)
                        if not last:
                            copy_attn_T(c + 1, u)
                    if last:
                        x_low(f, 0)
                    for u in range(CHUNK):
                        past(dve, s.x_added, t0 + u + 1)
                        nc.vector.bn_stats(stats[:, ds(t0 + u, 1), :].rearrange("p x n -> p (x n)"),
                                           x_tile(t0 + u)).then_inc(ln.stats, 1)

                for u in range(CHUNK):
                    copy_attn_T(0, u)
                with dve.Fori(0, CHUNKS - 1) as c:
                    chunk(c)
                aggregate(ln, EARLY)
                chunk(CHUNKS - 1, last=True)
                aggregate(ln, LATE_OF[EARLY])

            def feed_forward(f, ln_own, ln, q):
                def h_low(c, m):
                    dve.wait_ge(f.h_high, MC * c + m + 1)
                    nc.vector.tensor_tensor(h_split[1][:, m, :], h_sb[:, m % 2, :], h_split[0][:, m, :].bitcast(F32),
                                            ALU.subtract).then_inc(f.h_low, 1)

                def chunk(c, last=False):
                    for m in range(MC):
                        dve.wait_ge(f.silu_done, MC * c + m + 1)
                        past(dve, f.h_low, MC * c + max(0, m - 1))
                        nc.vector.tensor_tensor(h_sb[:, m % 2, :], gate_sb[:, m % 2, :], PS[:, 3 + 2 * (m % 2), :],
                                                ALU.mult).then_inc(f.h_ready, 1)
                        if m > 0:
                            h_low(c, m - 1)
                        if 0 < m <= CHUNK and not last:
                            norm_ffn(f, c + 1, m - 1)
                        if last and ln is not None and m == 1:
                            aggregate(ln, EARLY)
                        if last and ln is not None and m == 5:
                            dve.wait_ge(f.xt_ready, KC * CHUNKS)
                            factors(ln, EARLY)
                        if last and ln is not None and m >= 6:
                            for u in range(2):
                                norm_qkv(q, 0, 2 * (m - 6) + u)
                    h_low(c, MC - 1)
                    if not last:
                        x_low(f, c + 1)
                    for u in range(CHUNK):
                        t = c * CHUNK + u
                        past(dve, f.y_ready, t + 1)
                        nc.vector.tensor_tensor(x_tile(t), x_tile(t), PS[:, 6 + u % 2, 0:DIM],
                                                ALU.add).then_inc(f.x_added, 1)
                        if ln is not None:
                            past(dve, f.x_added, t + 1)
                            nc.vector.bn_stats(stats[:, ds(t, 1), :].rearrange("p x n -> p (x n)"),
                                               x_tile(t)).then_inc(ln.stats, 1)

                factors(ln_own, LATE_OF[EARLY])
                with dve.Fori(0, CHUNKS - 1) as c:
                    chunk(c)
                chunk(CHUNKS - 1, last=True)
                if ln is not None:
                    aggregate(ln, LATE_OF[EARLY])

            def stats_of_input(tiles):
                for t in range(*tiles):
                    if t % CHUNK == 0:
                        dve.wait_ge(s_x[t // CHUNK], 16)
                    nc.vector.bn_stats(stats[:, t, :], x[:, t, :]).then_inc(LN[0].stats, 1)
                aggregate(LN[0], tiles)
                factors(LN[0], tiles)

            stats_of_input(FIRST)
            for u in range(CHUNK):
                norm_qkv(QKV["a"], 0, u)
            stats_of_input(LATE_OF[FIRST])
            dve.wait_ge(s_in.rope, 16)
            qkv(A, QKV["a"])
            attention(A, ATT["a"], QKV["a"])
            out_projection(WO["a"], LN[1], False, FFN[0])
            feed_forward(FFN[0], LN[1], LN[2], QKV["b"])
            dve.wait_ge(s_in.bias, 64)
            qkv(B, QKV["b"])
            attention(B, ATT["b"], QKV["b"])
            out_projection(WO["b"], LN[3], True, FFN[1])
            feed_forward(FFN[1], LN[3], None, None)

        @block.tensor
        def _(pe):
            for q in (QKV["a"], QKV["b"]):
                open_counts(pe, q.xt_ready, q.qkv_ready, q.pt_ready)
            for s in (WO["a"], WO["b"]):
                open_counts(pe, s.t_ready, s.y_ready)
            for f in FFN:
                open_counts(pe, f.y_ready)
            pe.wait_ge(s_in.const, 4)
            pe.wait_ge(s_in.wa, 16 * 3)

            def transpose_tile(q, t0, u):
                pe.wait_ge(q.xn_ready, t0 + u + 1)
                past(pe, q.xnT_ready, t0 + max(0, u - 1))
                for k in range(KC):
                    last = nc.tensor.transpose(PS[:, u % 2, k * P:(k + 1) * P],
                                               xn[:, u % CHUNK, k * P:(k + 1) * P], ident[:, :])
                last.then_inc(q.xt_ready, 1)

            def qkv(L, q, w):
                def project(t0, u):
                    past(pe, q.xnT_ready, t0 + u + 1)
                    past(pe, q.rotated if L.bias else q.qk_read, t0 + max(0, u - 1))
                    past(pe, q.v_read, t0 + max(0, u - 1))
                    pieces = [(0, 0, L.nqk), (1, L.nqk, L.nv)] if L.bias else [(0, 0, L.nqk + L.nv)]
                    slot = u % CHUNK
                    for bank, n0, n in pieces:
                        for k in range(KC):
                            last = nc.tensor.matmul(PS[:, 2 + 2 * (u % 2) + bank, 0:n],
                                                    xnT[:, k, slot * P:(slot + 1) * P], w[:, k, n0:n0 + n],
                                                    start=(k == 0), stop=(k == KC - 1))
                    last.then_inc(q.qkv_ready, 1)

                def transpose_parts(t0, u):
                    n = L.blocks // L.batches
                    past(pe, q.parts_ready, t0 + u + 1)
                    for k in range(L.batches):
                        b = u * L.batches + k
                        past(pe, q.pt_copied, t0 * L.batches + max(0, b - 1))
                        for i in range(n):
                            last = nc.tensor.transpose(PSB[:, 6 + b % 2, i * P:(i + 1) * P],
                                                       parts[:, u % 2, (k * n + i) * P:(k * n + i + 1) * P],
                                                       ident_b[:, :])
                        last.then_inc(q.pt_ready, 1)

                def chunk(t0, last=False):
                    for u in range(CHUNK):
                        if not last or u + 2 < CHUNK:
                            project(t0, u + 2)
                        if not last:
                            transpose_tile(q, t0, u + 4)
                        transpose_parts(t0, u)

                project(0, 0)
                transpose_tile(q, 0, 2)
                transpose_tile(q, 0, 3)
                project(0, 1)
                with pe.Fori(0, CHUNKS - 1) as c:
                    chunk(c * CHUNK)
                chunk((CHUNKS - 1) * CHUNK, last=True)

            def transpose_weights(banks):
                for n in banks:
                    wait(pe, s_in.raw_copied, n - 3)
                    for i, src in enumerate(WEIGHT_BANKS_OF[n]):
                        last = nc.tensor.transpose(PS[:, n % 4, i * P:(i + 1) * P], src, ident[:, :])
                    last.then_inc(s_in.raw_T, 1)

            def attention(L, s, q):
                def QTg(g):
                    return QT[:, ds(g % 3, 1), :].rearrange("p x n -> p (x n)")

                def KTg(g):
                    return KT[:, ds(g % 3, 1), :].rearrange("p x n -> p (x n)")

                def k_head(h):
                    return h if L.kh > 1 else 0

                def scores(g, units):
                    qt, kt = QTg(g), KTg(g)
                    for n in units:
                        if n == 0:
                            wait(pe, s.loaded, 16 * L.loads * (g + 1))
                        i, which, heads, k0, w = UNITS[n]
                        wait(pe, s.s_reduced, len(UNITS) * g + n - 1)
                        for x0, h in enumerate(heads):
                            dst = PS[:, 4 + n % 2, x0 * w:(x0 + 1) * w]
                            diagonal = k0 + w == (i + 1) * P
                            kcol = k_head(h) * SEQ + k0
                            last = nc.tensor.matmul(dst, qt[0:MROW, h * SEQ + i * P:h * SEQ + (i + 1) * P],
                                                    kt[0:MROW, kcol:kcol + w], start=True, stop=not diagonal)
                            if diagonal:
                                last = nc.tensor.matmul(dst[:, w - P:w], ident_b[:, :], mask_b[:, :],
                                                        start=False, stop=True)
                        last.then_inc(s.s_ready, 1)

                def scores_T(g, step, half):
                    c, j = CHUNK_STEP[step]
                    off = max(0, j - 4 * c) * P
                    qt, kt = QTg(g), KTg(g)
                    if step == 0 and half == 0:
                        wait(pe, s.m_loaded, 16 * (g + 1))
                    wait(pe, s.exp_done, 2 * STEPS * g + 2 * step + half - 1)
                    for h in (2 * half, 2 * half + 1):
                        kcol, qcol = k_head(h) * SEQ + j * P, h * SEQ + c * NT
                        last = nc.tensor.matmul(PS[:, h, off:NT], kt[:, kcol:kcol + P], qt[:, qcol + off:qcol + NT],
                                                start=True, stop=True)
                    last.then_inc(s.st_ready, 1)

                def weigh(g, step):
                    c, j = CHUNK_STEP[step]
                    off = max(0, j - 4 * c) * P
                    if step == 0:
                        wait(pe, s.v_staged, g + 1)
                    if j == 0:
                        wait(pe, s.o_copied, 2 * g + c)
                    if step in DIAGONAL:
                        wait(pe, s.masked, len(DIAGONAL) * g + DIAGONAL.index(step) + 1)
                    else:
                        wait(pe, s.exp_done, 2 * STEPS * g + 2 * step + 2)
                    for h in range(HG):
                        last = nc.tensor.matmul(PS[32 * h:32 * (h + 1), 6, off:NT], v_st[:, j, k_head(h), :],
                                                PT[:, step % 3, h, off:NT], start=(j == 0), stop=(j == 4 * c + 3))
                    last.then_inc(s.pv_done, 1)

                def transpose_o(g, c):
                    wait(pe, s.o_copied, 2 * g + c + 1)
                    if c == 0:
                        wait(pe, s.normed, 2 * g)
                    elif isinstance(g, int) and g == L.groups - 1:
                        wait(pe, s.normed, 2 * g + 1)
                    else:
                        wait(pe, s.mT_copied, g + 2)
                    for i in range(4):
                        last = nc.tensor.transpose(PS[:, 7, i * P:(i + 1) * P], o_sb[:, i * P:(i + 1) * P], ident[:, :])
                    last.then_inc(s.ot_ready, 1)

                def transpose_max(g):
                    wait(pe, s.neg_ready, g + 1)
                    wait(pe, s.normed, 2 * g - 1)
                    nc.tensor.transpose(PSB[0:PARTS * HG * QB, 7, 0:P], neg_m[:, :, :, :].rearrange("p r h i -> p (r h i)"),
                                        ident_b[:, :]).then_inc(s.mT_ready, 1)

                def group(g, first=False, one_ahead=True, two_ahead=True):
                    for step in range(STEPS):
                        ahead = g + 1 if step < STEPS - LEAD else g + 2
                        units = UNIT_RUNS[(step + LEAD) % STEPS]
                        if not (one_ahead if step < STEPS - LEAD else two_ahead):
                            units = []
                        if first:
                            ahead, units = FIRST_RUNS[step]
                        scores_T(g, step, 0)
                        scores(ahead, units[0:1])
                        scores_T(g, step, 1)
                        scores(ahead, units[1:2])
                        if step >= BEHIND:
                            weigh(g, step - BEHIND)
                        elif not first:
                            weigh(g - 1, step - BEHIND + STEPS)
                        scores(ahead, units[2:])
                        if step == 2 and not first:
                            transpose_o(g - 1, 1)
                        if step == 6:
                            transpose_o(g, 0)
                        if step == MT_STEP and one_ahead:
                            transpose_max(g + 1)

                past(pe, q.rotated if L.bias else q.qk_read, TILES)
                past(pe, q.v_read, TILES)
                if L is A:
                    pe.wait_ge(s_in.wo_a, 16)
                    pe.wait_ge(s_in.wgu, 32)
                    pe.wait_ge(s_in.wb, 64)
                for n in range(len(UNITS)):
                    scores(0, [n])
                    if L is A:
                        transpose_weights(range(n, min(n + 1, len(WEIGHT_BANKS_OF))))
                past(pe, q.pt_copied, TILES * L.batches)
                transpose_max(0)
                scores(1, range(BEFORE))
                group(0, first=True)
                with pe.Fori(1, L.groups - 2) as g:
                    group(g)
                group(L.groups - 2, two_ahead=False)
                group(L.groups - 1, one_ahead=False, two_ahead=False)
                for step in range(STEPS - BEHIND, STEPS):
                    weigh(L.groups - 1, step)
                transpose_o(L.groups - 1, 1)

            def out_projection(s, w):
                def transpose_attn(c):
                    for u in range(CHUNK):
                        pe.wait_ge(s.at_ready, c * CHUNK + u + 1)
                        wait(pe, s.atT_ready, (c - 1) * CHUNK + u + 1)
                        for k in range(KC):
                            last = nc.tensor.transpose(PS[:, u, k * P:(k + 1) * P], xn[:, u, k * P:(k + 1) * P], ident[:, :])
                        last.then_inc(s.t_ready, 1)

                def chunk(c, last_chunk=False):
                    if not last_chunk:
                        transpose_attn(c + 1)
                    pe.wait_ge(s.atT_ready, c * CHUNK + CHUNK)
                    past(pe, s.x_added, c * CHUNK)
                    for u in range(CHUNK):
                        for k in range(KC):
                            last = nc.tensor.matmul(PS[:, 4 + u, 0:DIM], xnT[:, k, u * P:(u + 1) * P], w[:, k, :],
                                                    start=(k == 0), stop=(k == KC - 1))
                        last.then_inc(s.y_ready, 1)

                transpose_attn(0)
                with pe.Fori(0, CHUNKS - 1) as c:
                    chunk(c)
                chunk(CHUNKS - 1, last_chunk=True)

            def feed_forward(f, wo, q):
                def split_products(w, xs, out, start, stop):
                    for a, b in ((0, 0), (0, 1), (1, 0)):
                        mm = nc.tensor.matmul(out, w[a], xs[b], start=start and a + b == 0, stop=stop and a == 1)
                    return mm

                def transpose_x(c):
                    past(pe, f.x_low, KC * c)
                    for k in range(KC):
                        for u in range(CHUNK):
                            if k == 0:
                                pe.wait_ge(f.xn_ready, CHUNK * c + u + 1)
                            last = nc.tensor.transpose(PS[:, k, u * P:(u + 1) * P], xn[:, u, k * P:(k + 1) * P],
                                                       ident[:, :])
                        last.then_inc(f.xt_ready, 1)

                def gate_up(c):
                    for m in range(MC):
                        past(pe, f.h_ready, MC * c + max(0, m - 1))
                        for half in range(2):
                            col = half * INTER + m * P
                            for k in range(KC):
                                if m == 0 and half == 0:
                                    past(pe, f.x_low, KC * c + k + 1)
                                last = split_products([w[:, k, col:col + P] for w in w_gu_split],
                                                      [v[:, k, :] for v in xnT_split],
                                                      PS[:, 2 + 2 * (m % 2) + half, :], k == 0, k == KC - 1)
                        last.then_inc(f.gu_ready, 1)

                def down(c):
                    for u in range(CHUNK):
                        past(pe, f.x_added, CHUNK * c + max(0, u - 1))
                        for m in range(MC):
                            if u == 0:
                                past(pe, f.h_low, MC * c + m + 1)
                            last = split_products([h[:, m, u * P:(u + 1) * P] for h in h_split],
                                                  [w[:, m, :] for w in w_dn_split],
                                                  PS[:, 6 + u % 2, 0:DIM], m == 0, m == MC - 1)
                        last.then_inc(f.y_ready, 1)

                transpose_x(0)
                pe.wait_ge(wo.split_low, CHUNKS * SPLITS)
                with pe.Fori(0, CHUNKS - 1) as c:
                    gate_up(c)
                    transpose_x(c + 1)
                    down(c)
                gate_up(CHUNKS - 1)
                if q is not None:
                    transpose_tile(q, 0, 0)
                    transpose_tile(q, 0, 1)
                down(CHUNKS - 1)

            transpose_tile(QKV["a"], 0, 0)
            transpose_tile(QKV["a"], 0, 1)
            qkv(A, QKV["a"], w_qkv_a)
            attention(A, ATT["a"], QKV["a"])
            out_projection(WO["a"], w_out_a)
            feed_forward(FFN[0], WO["a"], QKV["b"])
            qkv(B, QKV["b"], w_qkv_b)
            attention(B, ATT["b"], QKV["b"])
            out_projection(WO["b"], w_out_b)
            feed_forward(FFN[1], WO["b"], None)


_INS = ["L0_attn_a_x", "L0_attn_a_wq", "L0_attn_a_wk", "L0_attn_a_wv", "L0_attn_a_wo",
        "L0_attn_b_Wq", "L0_attn_b_bq", "L0_attn_b_Wk", "L0_attn_b_bk", "L0_attn_b_Wv", "L0_attn_b_bv",
        "L0_attn_b_Wo", "L0_attn_b_bo", "L0_ffn_w_gate_up", "L0_ffn_w_down"]


def _rope_table(seq, d, theta=10000.0):
    import numpy as np

    freq = (np.float32(theta) ** (-(np.arange(d // 2, dtype=np.float32) * np.float32(2.0 / d)))).astype(np.float32)
    phase = np.arange(seq, dtype=np.float32)[:, None] * freq[None, :]
    cos, sin = np.cos(phase), np.sin(phase)
    table = np.concatenate([np.repeat(cos, 2, axis=1), np.stack([-sin, sin], axis=-1).reshape(seq, d)], axis=1)
    return np.ascontiguousarray(table.astype(np.float32))


def kernel(**inputs):
    import numpy as np
    import concourse.bacc as bacc
    from concourse.bass_utils import run_bass_kernel_spmd

    nc = bacc.Bacc("TRN2", target_bir_lowering=False, num_devices=1)
    arrays = {f"in_{n}": np.ascontiguousarray(inputs[n]) for n in _INS}
    arrays["rope_table"] = _rope_table(SEQ, DIM // 32)
    args = [nc.dram_tensor(n, a.shape, mybir.dt.from_np(a.dtype), kind="ExternalInput").ap()
            for n, a in arrays.items()]
    out = nc.dram_tensor("out", (BATCH, SEQ, DIM), F32, kind="ExternalOutput").ap()
    hybrid_layer(nc, *args, out)
    return run_bass_kernel_spmd(nc, [arrays], core_ids=[0]).results[0]["out"]
```
